# Optimizing a Trainium2 kernel written in Bass

```python
import numpy as np
import jax
import jax.numpy as jnp

def _softmax(x, axis=-1):
    return jax.nn.softmax(x, axis=axis)

def _gelu(x):
    return jax.nn.gelu(x, approximate=True)

def _silu(x):
    return jax.nn.silu(x)

def _sigmoid(x):
    return jax.nn.sigmoid(x)

def _layernorm(x, axis=-1, eps=1e-05):
    m = jnp.mean(x, axis=axis, keepdims=True)
    v = jnp.var(x, axis=axis, keepdims=True)
    return (x - m) / jnp.sqrt(v + eps)

def _scatter_add(tgt, idx, src, axis=0):
    return tgt.at[idx].add(src)

def _segment_sum(src, seg, n):
    return jax.ops.segment_sum(src, seg, n)
kernel_name = 'mk_dlrm_tower_d1_rec_r8_1a6e3d'

def setup_inputs(seed: int=0):
    np.random.seed(seed)
    _w = jnp.asarray

    def _rec_inputs():
        import jax
        import jax.numpy as jnp
        _tk = jax.random.key(seed)
        ids = jnp.stack([jax.random.randint(jax.random.fold_in(_tk, 200 + f), (2048,), 0, v, jnp.int32) for f, v in enumerate([1250, 1250, 1000, 1000, 1000, 1000, 1250, 125000, 12500, 1000, 1250, 12500, 1000, 1250, 12500, 1250, 12500, 1000, 12500, 12500, 12500, 1000, 1250, 1250, 1000, 1000])], axis=1)
        tbl_0 = 0.05 * jax.random.normal(jax.random.fold_in(_tk, 500 + 0), (1250, 128), jnp.float32)
        tbl_1 = 0.05 * jax.random.normal(jax.random.fold_in(_tk, 500 + 1), (1250, 128), jnp.float32)
        tbl_2 = 0.05 * jax.random.normal(jax.random.fold_in(_tk, 500 + 2), (1000, 128), jnp.float32)
        tbl_3 = 0.05 * jax.random.normal(jax.random.fold_in(_tk, 500 + 3), (1000, 128), jnp.float32)
        tbl_4 = 0.05 * jax.random.normal(jax.random.fold_in(_tk, 500 + 4), (1000, 128), jnp.float32)
        tbl_5 = 0.05 * jax.random.normal(jax.random.fold_in(_tk, 500 + 5), (1000, 128), jnp.float32)
        tbl_6 = 0.05 * jax.random.normal(jax.random.fold_in(_tk, 500 + 6), (1250, 128), jnp.float32)
        tbl_7 = 0.05 * jax.random.normal(jax.random.fold_in(_tk, 500 + 7), (125000, 128), jnp.float32)
        tbl_8 = 0.05 * jax.random.normal(jax.random.fold_in(_tk, 500 + 8), (12500, 128), jnp.float32)
        tbl_9 = 0.05 * jax.random.normal(jax.random.fold_in(_tk, 500 + 9), (1000, 128), jnp.float32)
        tbl_10 = 0.05 * jax.random.normal(jax.random.fold_in(_tk, 500 + 10), (1250, 128), jnp.float32)
        tbl_11 = 0.05 * jax.random.normal(jax.random.fold_in(_tk, 500 + 11), (12500, 128), jnp.float32)
        tbl_12 = 0.05 * jax.random.normal(jax.random.fold_in(_tk, 500 + 12), (1000, 128), jnp.float32)
        tbl_13 = 0.05 * jax.random.normal(jax.random.fold_in(_tk, 500 + 13), (1250, 128), jnp.float32)
        tbl_14 = 0.05 * jax.random.normal(jax.random.fold_in(_tk, 500 + 14), (12500, 128), jnp.float32)
        tbl_15 = 0.05 * jax.random.normal(jax.random.fold_in(_tk, 500 + 15), (1250, 128), jnp.float32)
        tbl_16 = 0.05 * jax.random.normal(jax.random.fold_in(_tk, 500 + 16), (12500, 128), jnp.float32)
        tbl_17 = 0.05 * jax.random.normal(jax.random.fold_in(_tk, 500 + 17), (1000, 128), jnp.float32)
        tbl_18 = 0.05 * jax.random.normal(jax.random.fold_in(_tk, 500 + 18), (12500, 128), jnp.float32)
        tbl_19 = 0.05 * jax.random.normal(jax.random.fold_in(_tk, 500 + 19), (12500, 128), jnp.float32)
        tbl_20 = 0.05 * jax.random.normal(jax.random.fold_in(_tk, 500 + 20), (12500, 128), jnp.float32)
        tbl_21 = 0.05 * jax.random.normal(jax.random.fold_in(_tk, 500 + 21), (1000, 128), jnp.float32)
        tbl_22 = 0.05 * jax.random.normal(jax.random.fold_in(_tk, 500 + 22), (1250, 128), jnp.float32)
        tbl_23 = 0.05 * jax.random.normal(jax.random.fold_in(_tk, 500 + 23), (1250, 128), jnp.float32)
        tbl_24 = 0.05 * jax.random.normal(jax.random.fold_in(_tk, 500 + 24), (1000, 128), jnp.float32)
        tbl_25 = 0.05 * jax.random.normal(jax.random.fold_in(_tk, 500 + 25), (1000, 128), jnp.float32)
        _rk = jax.random.fold_in(_tk, 7)
        r_dense_x = -0.000514642 + 1.00011 * jax.random.normal(jax.random.fold_in(_rk, 101), (2048, 128), jnp.float32)
        W_top1 = 0.0456912 * jax.random.normal(jax.random.fold_in(_tk, 801), (479, 512), jnp.float32)
        W_top2 = 0.0441942 * jax.random.normal(jax.random.fold_in(_tk, 802), (512, 256), jnp.float32)
        W_top3 = 0.0625 * jax.random.normal(jax.random.fold_in(_tk, 803), (256, 1), jnp.float32)
        b_top1 = jnp.zeros((512,), jnp.float32)
        b_top2 = jnp.zeros((256,), jnp.float32)
        return (r_dense_x, ids, tbl_0, tbl_1, tbl_2, tbl_3, tbl_4, tbl_5, tbl_6, tbl_7, tbl_8, tbl_9, tbl_10, tbl_11, tbl_12, tbl_13, tbl_14, tbl_15, tbl_16, tbl_17, tbl_18, tbl_19, tbl_20, tbl_21, tbl_22, tbl_23, tbl_24, tbl_25, W_top1, b_top1, W_top2, b_top2, W_top3)
    r_dense_x, ids, tbl_0, tbl_1, tbl_2, tbl_3, tbl_4, tbl_5, tbl_6, tbl_7, tbl_8, tbl_9, tbl_10, tbl_11, tbl_12, tbl_13, tbl_14, tbl_15, tbl_16, tbl_17, tbl_18, tbl_19, tbl_20, tbl_21, tbl_22, tbl_23, tbl_24, tbl_25, W_top1, b_top1, W_top2, b_top2, W_top3 = _rec_inputs()

    def _L0_rec_setup():
        import jax, jax.numpy as jnp
        import numpy as np
        F = 26
        D = 128
        B = 2048
        _TRIU_I, _TRIU_J = np.triu_indices(F + 1, k=1)
        _TRIU_I = jnp.asarray(_TRIU_I)
        _TRIU_J = jnp.asarray(_TRIU_J)
        key = jax.random.key(seed)
        k1, k2 = jax.random.split(key)
        sparse_x = jax.random.normal(k1, (B, F, D), dtype=jnp.float32)
        dense_x = jax.random.normal(k2, (B, D), dtype=jnp.float32)
        return {'sparse_x': sparse_x, 'dense_x': dense_x}
    _L0_rec_all = _L0_rec_setup()
    _L0_rec_in = {k: v for k, v in _L0_rec_all.items() if k in ()}
    del _L0_rec_all
    return {'r_dense_x': r_dense_x, 'ids': ids, 'tbl_0': tbl_0, 'tbl_1': tbl_1, 'tbl_2': tbl_2, 'tbl_3': tbl_3, 'tbl_4': tbl_4, 'tbl_5': tbl_5, 'tbl_6': tbl_6, 'tbl_7': tbl_7, 'tbl_8': tbl_8, 'tbl_9': tbl_9, 'tbl_10': tbl_10, 'tbl_11': tbl_11, 'tbl_12': tbl_12, 'tbl_13': tbl_13, 'tbl_14': tbl_14, 'tbl_15': tbl_15, 'tbl_16': tbl_16, 'tbl_17': tbl_17, 'tbl_18': tbl_18, 'tbl_19': tbl_19, 'tbl_20': tbl_20, 'tbl_21': tbl_21, 'tbl_22': tbl_22, 'tbl_23': tbl_23, 'tbl_24': tbl_24, 'tbl_25': tbl_25, 'W_top1': W_top1, 'b_top1': b_top1, 'W_top2': W_top2, 'b_top2': b_top2, 'W_top3': W_top3}

def reference(r_dense_x, ids, tbl_0, tbl_1, tbl_2, tbl_3, tbl_4, tbl_5, tbl_6, tbl_7, tbl_8, tbl_9, tbl_10, tbl_11, tbl_12, tbl_13, tbl_14, tbl_15, tbl_16, tbl_17, tbl_18, tbl_19, tbl_20, tbl_21, tbl_22, tbl_23, tbl_24, tbl_25, W_top1, b_top1, W_top2, b_top2, W_top3):
    import jax
    import jax.numpy as jnp

    def _L0_rec_ref(sparse_x, dense_x):
        import jax, jax.numpy as jnp
        import numpy as np
        F = 26
        D = 128
        B = 2048
        _TRIU_I, _TRIU_J = np.triu_indices(F + 1, k=1)
        _TRIU_I = jnp.asarray(_TRIU_I)
        _TRIU_J = jnp.asarray(_TRIU_J)
        combined = jnp.concatenate([sparse_x, dense_x[:, None, :]], axis=1)
        interact = jnp.einsum('bfd,bgd->bfg', combined, combined)
        return interact[:, _TRIU_I, _TRIU_J]
    e = jnp.stack([tbl_0[ids[:, 0]], tbl_1[ids[:, 1]], tbl_2[ids[:, 2]], tbl_3[ids[:, 3]], tbl_4[ids[:, 4]], tbl_5[ids[:, 5]], tbl_6[ids[:, 6]], tbl_7[ids[:, 7]], tbl_8[ids[:, 8]], tbl_9[ids[:, 9]], tbl_10[ids[:, 10]], tbl_11[ids[:, 11]], tbl_12[ids[:, 12]], tbl_13[ids[:, 13]], tbl_14[ids[:, 14]], tbl_15[ids[:, 15]], tbl_16[ids[:, 16]], tbl_17[ids[:, 17]], tbl_18[ids[:, 18]], tbl_19[ids[:, 19]], tbl_20[ids[:, 20]], tbl_21[ids[:, 21]], tbl_22[ids[:, 22]], tbl_23[ids[:, 23]], tbl_24[ids[:, 24]], tbl_25[ids[:, 25]]], axis=1)
    z = _L0_rec_ref(e, r_dense_x)
    z = z.reshape(z.shape[0], -1)
    h = jnp.concatenate([z, r_dense_x], axis=1)
    h = jnp.maximum(h @ W_top1 + b_top1, 0.0)
    h = jnp.maximum(h @ W_top2 + b_top2, 0.0)
    y = h @ W_top3
    return y

_drawn_inputs = setup_inputs


def setup_inputs(seed=0):
    import zlib

    import numpy as np

    out = dict(_drawn_inputs(seed))
    spreads = {'b_top1': (0.0, 0.1), 'b_top2': (0.0, 0.1)}
    factors = {}
    for name, (base, spread) in spreads.items():
        noise = np.random.default_rng([zlib.crc32(name.encode()), seed]).standard_normal(out[name].shape)
        drawn = base * np.exp(spread * noise) if base else spread * noise
        out[name] = jnp.asarray(drawn.astype(out[name].dtype))
    for name, factor in factors.items():
        out[name] = (out[name] * factor).astype(out[name].dtype)
    return out
```

```python
import concourse.bass as bass
from concourse import mybir
from contextlib import ExitStack


def dlrm_tower_kernel(nc, x, ids, tables, w1, b1, w2, b2, w3, out):
    fp32 = mybir.dt.float32
    f32r = mybir.dt.float32r
    i32 = mybir.dt.int32
    u32 = mybir.dt.uint32
    ALU = mybir.AluOpType
    ACT = mybir.ActivationFunctionType

    B, D = x.shape
    NT = len(tables)
    F = NT + 1
    TILE = 128
    SUPER = 4
    TURNS = B // (TILE * SUPER)
    AHEAD = 2
    UNIT = 2
    UNITS = SUPER // UNIT
    COLS = TILE * SUPER
    FP = 32
    FM = 28
    S = 4
    GT = TILE // S
    GB = 4
    BANK = 512
    BATCH = 2 * GB
    BATCHES = UNIT * GT // BATCH
    PAIRS = F * (F - 1) // 2
    ZC = 3
    ZR = PAIRS // ZC
    H1 = w1.shape[1]
    H2 = w2.shape[1]
    N1 = H1 // 128
    N2 = H2 // 128
    GROUPS = [(g, min(4, F - g)) for g in range(0, F, 4)]
    NG = len(GROUPS)
    MB = [(j, min(4, F - j)) for j in range(0, F, 4)]

    ctx = ExitStack()
    with ctx:
        def sb(name, shape, dt):
            return ctx.enter_context(nc.sbuf_tensor(name, shape, dt))

        def sem(name):
            return ctx.enter_context(nc.semaphore(name))

        idx = sb("idx", [128, AHEAD, NT], i32)
        emb = sb("emb", [128, AHEAD, F, D], fp32)
        ident = sb("ident", [128, 128], fp32)
        half = sb("half", [128, UNIT * TILE, FP], f32r)
        low = sb("low", [128, UNIT * TILE, FP], f32r)
        den_h = sb("den_h", [128, S, TILE], f32r)
        den_l = sb("den_l", [128, S, TILE], f32r)
        gram = sb("gram", [128, SUPER * GT, FM], fp32)
        full = sb("full", [128, F, S, FP], fp32)
        tri = sb("tri", [128, S, PAIRS], fp32)
        z_h = sb("z_h", [ZR, ZC, COLS], f32r)
        z_l = sb("z_l", [ZR, ZC, COLS], f32r)
        h1_x = sb("h1_x", [128, 2, COLS], fp32)
        h1_h = sb("h1_h", [128, N1, COLS], f32r)
        h1_l = sb("h1_l", [128, N1, COLS], f32r)
        h2 = sb("h2", [128, N2, COLS], fp32)
        y = sb("y", [1, 2, COLS], fp32)
        w_raw = full[:].rearrange("p j s f -> p (j s f)")
        w1z_raw = w_raw[:ZR, 0:ZC * H1].rearrange("p (c n) -> p c n", c=ZC)
        w1d_raw = w_raw[:, ZC * H1:(ZC + 1) * H1]
        w2_raw = w_raw[:, (ZC + 1) * H1:(ZC + 1) * H1 + N1 * H2].rearrange("p (c n) -> p c n", c=N1)
        w1z_h = sb("w1z_h", [ZR, ZC, H1], f32r)
        w1z_l = sb("w1z_l", [ZR, ZC, H1], f32r)
        w1d_h = sb("w1d_h", [128, H1], f32r)
        w1d_l = sb("w1d_l", [128, H1], f32r)
        w2_h = sb("w2_h", [128, N1, H2], f32r)
        w2_l = sb("w2_l", [128, N1, H2], f32r)
        w3_sb = sb("w3_sb", [128, N2], fp32)
        b1_sb = sb("b1_sb", [128, N1], fp32)
        b2_sb = sb("b2_sb", [128, N2], fp32)

        ps_in = ctx.enter_context(nc.psum_tensor("ps_in", [128, 2, BANK], fp32))
        ps_gr = ctx.enter_context(nc.psum_tensor("ps_gr", [128, 2, 2, BANK], fp32))
        ps_mx = ctx.enter_context(nc.psum_tensor("ps_mx", [128, 2, BANK], fp32))

        ids_in = [sem(f"ids_in{t}") for t in range(AHEAD)]
        dense_in = [sem(f"dense_in{t}") for t in range(AHEAD)]
        rows_in = [[sem(f"rows_in{t}_{g}") for g in range(NG)] for t in range(AHEAD)]
        emb_free = [sem(f"emb_free{t}") for t in range(AHEAD)]
        tile_begun = sem("tile_begun")
        weights_in = sem("weights_in")
        small_in = sem("small_in")
        zeroed = sem("zeroed")
        ident_zeroed = sem("ident_zeroed")
        ident_made = sem("ident_made")
        w_high = sem("w_high")
        w_split = sem("w_split")
        turned = sem("turned")
        half_made = sem("half_made")
        low_made = sem("low_made")
        gram_done = sem("gram_done")
        gram_act = sem("gram_act")
        gram_dve = sem("gram_dve")
        mid_done = sem("mid_done")
        mid_out = sem("mid_out")
        tri_made = sem("tri_made")
        z_done = sem("z_done")
        z_high = sem("z_high")
        z_low = sem("z_low")
        l1_done = sem("l1_done")
        h1_high = sem("h1_high")
        h1_full = sem("h1_full")
        h1_low = sem("h1_low")
        l2_done = sem("l2_done")
        h2_made = sem("h2_made")
        l3_done = sem("l3_done")
        y_made = sem("y_made")
        y_out = sem("y_out")
        block = ctx.enter_context(nc.Block())

        NB = SUPER * NG
        NGB = UNITS * BATCHES
        NMB = len(MB)
        SLOTS = 2

        MIX_ORDER = [("mid", k) for k in range(NMB)] + [("z", k) for k in range(ZC)] + \
                    [("l1", k) for k in range(N1)] + [("l2", k) for k in range(N2)] + [("l3", 0)]
        NMIX = len(MIX_ORDER)
        mix_slot = {what: n % SLOTS for n, what in enumerate(MIX_ORDER)}
        if NMIX % SLOTS:
            last_slot = mix_slot[("l3", 0)]
            assert last_slot == 0

        def gathered(w):
            first, n = GROUPS[w]
            return sum(f < NT for f in range(first, first + n))

        def own_block(k, s):
            src = ps_gr[s * FP:(s + 1) * FP, k % SLOTS, :, 0:GB * S * FM] \
                .rearrange("p b (g s j) -> p b g s j", g=GB, s=S)[:, :, :, s, :]
            dst = gram[s * FP:(s + 1) * FP, k * BATCH:(k + 1) * BATCH, :] \
                .rearrange("p (b g) j -> p b g j", b=2)
            return dst, src

        @block.sync
        def _(sp):
            sp.dma_start(w3_sb[:], w3[:, :]).then_inc(small_in, 16)
            sp.dma_start(b1_sb[:], b1[:, :]).then_inc(small_in, 16)
            sp.dma_start(b2_sb[:], b2[:, :]).then_inc(small_in, 16)
            with sp.Fori(0, TURNS) as i:
                for t in range(SUPER):
                    slot, turn = t % AHEAD, i * (SUPER // AHEAD) + t // AHEAD
                    sp.wait_ge(emb_free[slot], turn)
                    at = (i * SUPER + t) * TILE
                    sp.dma_start(idx[:, slot, :], ids[bass.ds(at, TILE), :]).then_inc(ids_in[slot], 16)
                    sp.dma_start(emb[:, slot, NT, :], x[bass.ds(at, TILE), :]).then_inc(dense_in[slot], 16)
                sp.wait_ge(y_made, i + 1)
                sp.dma_start(out[0:1, bass.ds(i * COLS, COLS)], y[0:1, 0, :]).then_inc(y_out, 16)
            sp.wait_ge(y_out, 16 * TURNS)

        @block.gpsimd
        def _(pool):
            pool.wait_ge(ident_zeroed, 1)
            nc.gpsimd.affine_select(out=ident[:], in_=ident[:], compare_op=ALU.not_equal, fill=1.0, base=0,
                                    pattern=[[-1, 128]], channel_multiplier=1).then_inc(ident_made, 1)
            with pool.Fori(0, TURNS) as i:
                for t in range(SUPER):
                    slot, turn = t % AHEAD, i * (SUPER // AHEAD) + t // AHEAD
                    pool.wait_ge(ids_in[slot], 16 * (turn + 1))
                    pool.wait_ge(emb_free[slot], turn)
                    pool.sem_inc(tile_begun, 1)
                    for f in range(NT):
                        pool.indirect_dma_start(
                            emb[:, slot, f, :], None, tables[f],
                            bass.IndirectOffsetOnAxis(ap=idx[:, slot, f:f + 1].bitcast(u32), axis=0),
                        ).then_inc(rows_in[slot][f // 4], 16)

        @block.tensor
        def _(pe):
            pe.wait_ge(ident_made, 1)
            pe.wait_ge(zeroed, 1)
            pe.wait_ge(small_in, 48)
            pe.wait_ge(w_split, 3)
            with pe.Fori(0, TURNS) as i:
                for u in range(UNITS):
                    for h in range(UNIT):
                        t = u * UNIT + h
                        slot, turn = t % AHEAD, i * (SUPER // AHEAD) + t // AHEAD
                        for w, (first, n) in enumerate(GROUPS):
                            k = t * NG + w
                            pe.wait_ge(rows_in[slot][w], 16 * gathered(w) * (turn + 1))
                            if first + n == F:
                                pe.wait_ge(dense_in[slot], 16 * (turn + 1))
                            if k >= SLOTS:
                                pe.wait_ge(low_made, i * NB + k - SLOTS + 1)
                            else:
                                pe.wait_ge(low_made, i * NB)
                            for f in range(n):
                                ins = nc.tensor.transpose(ps_in[:, k % SLOTS, f * TILE:(f + 1) * TILE],
                                                          emb[:, slot, first + f, :], ident[:])
                            ins.then_inc(turned, 1)
                    pe.wait_ge(low_made, i * NB + (u + 1) * UNIT * NG)
                    for b in range(BATCHES):
                        k = u * BATCHES + b
                        done = i * NGB + k - SLOTS + 1 if k >= SLOTS else i * NGB
                        pe.wait_ge(gram_act, done)
                        pe.wait_ge(gram_dve, done)
                        for q in range(BATCH):
                            s0 = (b * BATCH + q) * S
                            o = ps_gr[:, k % SLOTS, q // GB, (q % GB) * S * FM:(q % GB + 1) * S * FM]
                            nc.tensor.matmul(o, half[:, s0:s0 + S, :], half[:, s0:s0 + S, 0:FM],
                                             start=True, stop=False)
                            ins = nc.tensor.matmul(o, half[:, s0:s0 + S, :], low[:, s0:s0 + S, 0:FM],
                                                   start=False, stop=True)
                        ins.then_inc(gram_done, 1)
                pe.wait_ge(gram_act, (i + 1) * NGB)
                pe.wait_ge(gram_dve, (i + 1) * NGB)
                for m, (j0, n) in enumerate(MB):
                    if m >= SLOTS:
                        pe.wait_ge(mid_out, i * NMB + m - SLOTS + 1)
                    for j in range(n):
                        ins = nc.tensor.transpose(ps_mx[:, mix_slot[("mid", m)], j * 128:(j + 1) * 128],
                                                  gram[:, :, j0 + j], ident[:])
                    ins.then_inc(mid_done, 1)
                pe.wait_ge(mid_out, (i + 1) * NMB)
                pe.wait_ge(tri_made, i + 1)
                for c in range(ZC):
                    if c >= SLOTS:
                        pe.wait_ge(z_low, i * ZC + c - SLOTS + 1)
                    for s in range(S):
                        ins = nc.tensor.transpose(ps_mx[:ZR, mix_slot[("z", c)], s * 128:(s + 1) * 128],
                                                  tri[:, s, c * ZR:(c + 1) * ZR], ident[:])
                    ins.then_inc(z_done, 1)
                pe.wait_ge(z_low, (i + 1) * ZC)
                for n in range(N1):
                    if n >= SLOTS:
                        pe.wait_ge(h1_high, i * N1 + n - SLOTS + 1)
                    o = ps_mx[:, mix_slot[("l1", n)], :]
                    cols = slice(n * 128, (n + 1) * 128)
                    terms = [(w1d_h[:, cols], den_h[:, :, :]), (w1d_h[:, cols], den_l[:, :, :]),
                             (w1d_l[:, cols], den_h[:, :, :])]
                    for c in range(ZC):
                        terms += [(w1z_h[:, c, cols], z_h[:, c, :]), (w1z_h[:, c, cols], z_l[:, c, :]),
                                  (w1z_l[:, c, cols], z_h[:, c, :])]
                    for k, (w, v) in enumerate(terms):
                        ins = nc.tensor.matmul(o, w, v, start=k == 0, stop=k == len(terms) - 1)
                    ins.then_inc(l1_done, 1)
                pe.wait_ge(h1_low, (i + 1) * N1)
                for n in range(N2):
                    o = ps_mx[:, mix_slot[("l2", n)], :]
                    cols = slice(n * 128, (n + 1) * 128)
                    terms = []
                    for c in range(N1):
                        terms += [(w2_h[:, c, cols], h1_h[:, c, :]), (w2_h[:, c, cols], h1_l[:, c, :]),
                                  (w2_l[:, c, cols], h1_h[:, c, :])]
                    for k, (w, v) in enumerate(terms):
                        ins = nc.tensor.matmul(o, w, v, start=k == 0, stop=k == len(terms) - 1)
                    ins.then_inc(l2_done, 1)
                pe.wait_ge(h2_made, (i + 1) * N2)
                for c in range(N2):
                    ins = nc.tensor.matmul(ps_mx[0:1, mix_slot[("l3", 0)], :], w3_sb[:, c:c + 1], h2[:, c, :],
                                           start=c == 0, stop=c == N2 - 1)
                ins.then_inc(l3_done, 1)
                pe.wait_ge(y_made, i + 1)

        @block.scalar
        def _(act):
            act.dma_start(w1z_raw, w1[0:PAIRS, :].rearrange("(c p) n -> p c n", p=ZR)).then_inc(weights_in, 16)
            act.dma_start(w1d_raw, w1[PAIRS:PAIRS + D, :]).then_inc(weights_in, 16)
            act.dma_start(w2_raw, w2.rearrange("(c p) n -> p c n", p=128)).then_inc(weights_in, 16)
            act.wait_ge(weights_in, 48)
            nc.scalar.activation(w1z_h[:], w1z_raw, ACT.Copy, scale=2.0).then_inc(w_high, 1)
            nc.scalar.activation(w1d_h[:], w1d_raw, ACT.Copy).then_inc(w_high, 1)
            nc.scalar.activation(w2_h[:], w2_raw, ACT.Copy).then_inc(w_high, 1)
            act.wait_ge(small_in, 48)
            act.wait_ge(zeroed, 1)
            with act.Fori(0, TURNS) as i:
                for u in range(UNITS):
                    act.wait_ge(gram_done, i * NGB + u * BATCHES)
                    for h in range(UNIT):
                        for w, (first, n) in enumerate(GROUPS):
                            k = (u * UNIT + h) * NG + w
                            act.wait_ge(turned, i * NB + k + 1)
                            src = ps_in[:, k % SLOTS, 0:n * TILE].rearrange("d (f b) -> d f b", b=TILE)
                            if first + n == F:
                                g0 = (u * UNIT + h) * GT
                                nc.scalar.activation(
                                    den_h[:, :, g0:g0 + GT],
                                    src[:, n - 1, :].rearrange("d (g s) -> d s g", s=S), ACT.Copy
                                ).then_inc(emb_free[h % AHEAD], 1)
                            dst = half[:, h * TILE:(h + 1) * TILE, first:first + n].rearrange("d b f -> d f b")
                            nc.scalar.activation(dst, src, ACT.Copy, scale=0.5).then_inc(half_made, 1)
                    for b in range(BATCHES):
                        k = u * BATCHES + b
                        act.wait_ge(gram_done, i * NGB + k + 1)
                        for s in range(0, 2):
                            ins = nc.scalar.copy(*own_block(k, s))
                        ins.then_inc(gram_act, 1)
                for m, (j0, n) in enumerate(MB):
                    act.wait_ge(mid_done, i * NMB + m + 1)
                    nc.scalar.copy(full[:, j0:j0 + n, :, :].rearrange("p j s f -> p (j s f)"),
                                   ps_mx[:, mix_slot[("mid", m)], 0:n * 128]).then_inc(mid_out, 1)
                for c in range(ZC):
                    act.wait_ge(z_done, i * ZC + c + 1)
                    nc.scalar.copy(z_h[:, c, :], ps_mx[:ZR, mix_slot[("z", c)], :]).then_inc(z_high, 1)
                for n in range(N1):
                    act.wait_ge(h1_full, i * N1 + n + 1)
                    nc.scalar.activation(h1_h[:, n, :], ps_mx[:, mix_slot[("l1", n)], :], ACT.Relu,
                                         bias=b1_sb[:, n:n + 1]).then_inc(h1_high, 1)
                for n in range(N2):
                    act.wait_ge(l2_done, i * N2 + n + 1)
                    nc.scalar.activation(h2[:, n, :], ps_mx[:, mix_slot[("l2", n)], :], ACT.Relu,
                                         bias=b2_sb[:, n:n + 1]).then_inc(h2_made, 1)

        @block.vector
        def _(dve):
            nc.vector.memset(ident[:], 0.0).then_inc(ident_zeroed, 1)
            nc.vector.memset(half[:, :, F:FP].bitcast(fp32), 0.0)
            nc.vector.memset(low[:, :, F:FP].bitcast(fp32), 0.0).then_inc(zeroed, 1)
            dve.wait_ge(weights_in, 48)
            dve.wait_ge(w_high, 3)
            nc.vector.scalar_tensor_tensor(w1z_l[:], w1z_raw, 2.0, w1z_h[:].bitcast(fp32), ALU.mult,
                                           ALU.subtract).then_inc(w_split, 1)
            nc.vector.tensor_tensor(w1d_l[:], w1d_raw, w1d_h[:].bitcast(fp32), ALU.subtract).then_inc(w_split, 1)
            nc.vector.tensor_tensor(w2_l[:], w2_raw, w2_h[:].bitcast(fp32), ALU.subtract).then_inc(w_split, 1)
            dve.wait_ge(small_in, 48)
            with dve.Fori(0, TURNS) as i:
                for u in range(UNITS):
                    for h in range(UNIT):
                        for w, (first, n) in enumerate(GROUPS):
                            k = (u * UNIT + h) * NG + w
                            dve.wait_ge(half_made, i * NB + k + 1)
                            src = ps_in[:, k % SLOTS, 0:n * TILE].rearrange("d (f b) -> d f b", b=TILE)
                            if first + n == F:
                                g0 = (u * UNIT + h) * GT
                                nc.vector.tensor_tensor(
                                    den_l[:, :, g0:g0 + GT],
                                    src[:, n - 1, :].rearrange("d (g s) -> d s g", s=S),
                                    den_h[:, :, g0:g0 + GT].bitcast(fp32), ALU.subtract)
                            at = (slice(None), slice(h * TILE, (h + 1) * TILE), slice(first, first + n))
                            nc.vector.scalar_tensor_tensor(
                                low[at].rearrange("d b f -> d f b"),
                                half[at].rearrange("d b f -> d f b").bitcast(fp32), -2.0, src,
                                ALU.mult, ALU.add).then_inc(low_made, 1)
                    for b in range(BATCHES):
                        k = u * BATCHES + b
                        dve.wait_ge(gram_done, i * NGB + k + 1)
                        for s in range(2, S):
                            ins = nc.vector.tensor_copy(*own_block(k, s))
                        ins.then_inc(gram_dve, 1)
                dve.wait_ge(mid_out, (i + 1) * NMB)
                for j in range(1, F):
                    at = j * (j - 1) // 2
                    ins = nc.vector.tensor_tensor(tri[:, :, at:at + j], full[:, j, :, 0:j],
                                                  full[:, 0:j, :, j].rearrange("p a s -> p s a"), ALU.add)
                ins.then_inc(tri_made, 1)
                for c in range(ZC):
                    dve.wait_ge(z_high, i * ZC + c + 1)
                    nc.vector.tensor_tensor(z_l[:, c, :], ps_mx[:ZR, mix_slot[("z", c)], :],
                                            z_h[:, c, :].bitcast(fp32), ALU.subtract).then_inc(z_low, 1)
                for n in range(N1 + 1):
                    if n < N1:
                        dve.wait_ge(l1_done, i * N1 + n + 1)
                        dve.wait_ge(h1_low, i * N1 + max(n - 1, 0))
                        nc.vector.tensor_scalar(h1_x[:, n % 2, :], ps_mx[:, mix_slot[("l1", n)], :],
                                                b1_sb[:, n:n + 1], 0.0, ALU.add, ALU.max).then_inc(h1_full, 1)
                    if n > 0:
                        dve.wait_ge(h1_high, i * N1 + n)
                        dve.wait_ge(h1_full, i * N1 + n)
                        nc.vector.tensor_tensor(h1_l[:, n - 1, :], h1_x[:, (n - 1) % 2, :],
                                                h1_h[:, n - 1, :].bitcast(fp32), ALU.subtract).then_inc(h1_low, 1)
                dve.wait_ge(l3_done, i + 1)
                dve.wait_ge(y_out, 16 * i)
                nc.vector.tensor_copy(y[0:1, 0, :].rearrange("o (p s) -> o s p", s=S),
                                      ps_mx[0:1, mix_slot[("l3", 0)], :].rearrange("o (s p) -> o s p", s=S)
                                      ).then_inc(y_made, 1)


_INS = ["r_dense_x", "ids"] + [f"tbl_{t}" for t in range(26)] + ["W_top1", "b_top1", "W_top2", "b_top2", "W_top3"]


def kernel(**inputs):
    import numpy as _np
    import concourse.bacc as _bacc
    from concourse import mybir as _mybir
    from concourse.bass_utils import run_bass_kernel_spmd as _run

    nt = inputs["ids"].shape[1]
    lay = {name: _np.asarray(inputs[name]) for name in _INS}
    row = {}
    for a in range(nt + 1):
        for b in range(a + 1, nt + 1):
            row[a, b] = len(row)
    order = [row[a, b] for b in range(nt + 1) for a in range(b)]
    order += list(range(len(row), lay["W_top1"].shape[0]))
    lay["W_top1"] = lay["W_top1"][order]
    lay["b_top1"] = lay["b_top1"].reshape(-1, 128).T
    lay["b_top2"] = lay["b_top2"].reshape(-1, 128).T
    lay["W_top3"] = lay["W_top3"].reshape(-1, 128).T

    nc = _bacc.Bacc("TRN2", target_bir_lowering=False, num_devices=1)
    arrays, args = {}, []
    for name in _INS:
        a = _np.ascontiguousarray(lay[name])
        arrays[f"in_{name}"] = a
        args.append(nc.dram_tensor(f"in_{name}", a.shape, _mybir.dt.from_np(a.dtype), kind="ExternalInput").ap())
    rows = lay["r_dense_x"].shape[0]
    out = nc.dram_tensor("out_y", (1, rows), _mybir.dt.float32, kind="ExternalOutput").ap()
    x, ids, tables = args[0], args[1], args[2:2 + nt]
    w1, b1, w2, b2, w3 = args[2 + nt:]
    dlrm_tower_kernel(nc, x, ids, tables, w1, b1, w2, b2, w3, out)
    r = _run(nc, [arrays], core_ids=[0])
    return r.results[0]["out_y"].reshape(rows, 1)
```

```python
import concourse.bass as bass
from concourse import mybir
from contextlib import ExitStack


def dlrm_tower_kernel(nc, x, ids, ids_t, gathered, held, w1, b1, w2, b2, w3, out):
    fp32 = mybir.dt.float32
    f32r = mybir.dt.float32r
    i32 = mybir.dt.int32
    u32 = mybir.dt.uint32
    ALU = mybir.AluOpType
    ACT = mybir.ActivationFunctionType

    B, D = x.shape
    NG, NH = len(gathered), len(held)
    F = NG + 1 + NH
    DENSE = NG
    TILE = 128
    UNIT = 2
    UNITS = 2
    UC = UNIT * TILE
    COLS = UNITS * UC
    TURNS = B // COLS
    FP = 32
    S = 4
    BANK = 512
    GB = 4
    BATCHES = UC // S // GB
    GROUPS = COLS // S
    PAIRS = F * (F - 1) // 2
    ZC = 3
    ZR = PAIRS // ZC
    H1, H2 = w1.shape[1], w2.shape[1]
    N1, N2 = H1 // 128, H2 // 128
    ROWS = held[0][1].shape[0]
    HC = -(-ROWS // 128)
    HR = ROWS // HC
    BANKS = [(f, min(4, NG - f)) for f in range(0, NG, 4)]
    NB = len(BANKS)
    MID = [(j, min(4, F - j)) for j in range(0, F, 4)]
    NM = len(MID)
    MA, MV = (NM + 1) // 2, NM // 2

    assert NM == 7 and N1 == 4 and N2 == 2 and ZC * ZR == PAIRS and HC * HR == ROWS

    def merged(*spans):
        at = [(start + (end - start) * (n + 0.5) / len(steps), m, n, step)
              for m, (steps, start, end) in enumerate(spans) for n, step in enumerate(steps)]
        return [step for *_, step in sorted(at)]

    def steps(u, later):
        mid, z, l1, l2, l3 = ([(kind, k) for k in range(n)] if later else []
                              for kind, n in (("mid", NM), ("z", ZC), ("l1", N1), ("l2", N2), ("l3", 1)))
        rows = [("rows", w) for w in range(UNIT * NB)]
        held = [("held", o) for o in range(NH)]
        gram = [("gram", b) for b in range(BATCHES)]
        half = BATCHES // UNIT
        out = [("hot", 0), ("hot", 1)]
        for step in merged((rows[:NB], 0, 0.5), (held, 0.05, 1), (mid + z + l1 if u == 0 else l3, 0, 1)):
            out.append(step)
            if step[0] == "held" and step[1] + 2 < NH:
                out.append(("hot", step[1] + 2))
        out.append(("dense", 0))
        out += merged((rows[NB:], 0, 0.9), (gram[:half], 0.1, 1))
        return out + merged((gram[half:], 0, 1), (l2 if u == 0 else [], 0, 1))

    banks = [(u, *step) for u in range(UNITS) for step in steps(u, False)
             if step[0] in ("rows", "held", "dense")]
    NE = len(banks)
    nth = {bank: e for e, bank in enumerate(banks)}
    rings = {"in": [b for b in banks if b[1] != "held"], "held": [b for b in banks if b[1] == "held"]}
    slot_of, before = {}, {}
    for ring in rings.values():
        assert len(ring) % 2 == 0
        for r, bank in enumerate(ring):
            slot_of[bank] = r % 2
            before[bank] = (ring[r - 2], -1 if r < 2 else 0)

    def by_vector(kind, k):
        return kind == "rows" and k % 3 == 2

    act_nth, dve_nth = {}, {}
    for bank in banks:
        if not by_vector(*bank[1:]):
            act_nth[bank] = len(act_nth)
        if by_vector(*bank[1:]) or bank[1] == "dense":
            dve_nth[bank] = len(dve_nth)
    NA, NV = len(act_nth), len(dve_nth)

    mix_order = [("mid", m) for m in range(NM)] + [("z", c) for c in range(ZC)] + \
        [("l1", n) for n in range(N1)] + [("l2", n) for n in range(N2)] + [("l3", 0)]
    mix = {what: n % 2 for n, what in enumerate(mix_order)}

    ctx = ExitStack()
    with ctx:
        def sb(name, shape, dt):
            return ctx.enter_context(nc.sbuf_tensor(name, shape, dt))

        def sem(name):
            return ctx.enter_context(nc.semaphore(name))

        sizes = [GROUPS * F * 4, 2 * N1 * COLS * 4, (2 + N2) * COLS * 4]
        at_gram = -(-nc.sbuf_base // 32) * 32
        sb("shared", [128, sum(sizes) // 4], fp32)
        idx = sb("idx", [128, UNIT, NG + NH], i32)
        emb = sb("emb", [128, UNIT, NG, D], fp32)
        dense = sb("dense", [128, UNIT, D], fp32)
        ident = sb("ident", [128, 128], fp32)
        row_ids = sb("row_ids", [HR, HC], i32)
        ids_row = sb("ids_row", [HR, 2, UC], i32)
        hot = sb("hot", [HR, 2, HC, UC], f32r)
        held_h = sb("held_h", [HR, NH, HC, D], f32r)
        held_l = sb("held_l", [HR, NH, HC, D], f32r)
        feat = sb("feat", [128, UC, FP], fp32)
        feat_v = feat[:, :, :].rearrange("d b f -> d f b")
        den_h = sb("den_h", [128, S, GROUPS], f32r)
        den_l = sb("den_l", [128, S, GROUPS], f32r)
        y = sb("y", [1, COLS], fp32)
        w1z_h = sb("w1z_h", [ZR, ZC, H1], f32r)
        w1z_l = sb("w1z_l", [ZR, ZC, H1], f32r)
        w1d_h = sb("w1d_h", [128, H1], f32r)
        w1d_l = sb("w1d_l", [128, H1], f32r)
        w2_h = sb("w2_h", [128, N1, H2], f32r)
        w2_l = sb("w2_l", [128, N1, H2], f32r)
        w3_sb = sb("w3_sb", [128, N2], fp32)
        b1_sb = sb("b1_sb", [128, N1], fp32)
        b2_sb = sb("b2_sb", [128, N2], fp32)

        at_h1, at_tri, at_end = (at_gram + sum(sizes[:n]) for n in (1, 2, 3))
        placed = [at_gram, at_end]

        def place(name, shape, dt, at):
            size = 4
            for n in shape[1:]:
                size *= n
            assert placed[0] <= at and at + size <= placed[1]
            return nc.alloc_sbuf_tensor_at(name, shape, dt, offset=at)

        gram = place("gram", [128, GROUPS, F], fp32, at_gram)
        z_h = place("z_h", [ZR, ZC, COLS], f32r, at_gram)
        z_l = place("z_l", [ZR, ZC, COLS], f32r, at_gram + ZC * COLS * 4)
        h1_h = place("h1_h", [128, N1, COLS], f32r, at_h1)
        h1_l = place("h1_l", [128, N1, COLS], f32r, at_h1 + N1 * COLS * 4)
        tri = place("tri", [128, S, PAIRS], fp32, at_tri)
        h1_x = place("h1_x", [128, 2, COLS], fp32, at_tri)
        h2 = place("h2", [128, N2, COLS], fp32, at_tri + 2 * COLS * 4)
        held_raw = place("held_raw", [HR, NH, HC, D], fp32, at_gram)
        w1z_raw = sb("w1z_raw", [ZR, ZC, H1], fp32)
        w1d_raw = sb("w1d_raw", [128, H1], fp32)
        w2_raw = sb("w2_raw", [128, N1, H2], fp32)

        def ps(name, shape):
            return ctx.enter_context(nc.psum_tensor(name, shape, fp32))

        ps_in = ps("ps_in", [128, 2, BANK])
        ps_held = ps("ps_held", [128, 2, BANK])
        ps_gram = ps("ps_gram", [128, 2, BANK])
        ps_mix = ps("ps_mix", [128, 2, BANK])

        ids_in = [sem(f"ids_in{h}") for h in range(UNIT)]
        rows_in = [[sem(f"rows_in{h}_{w}") for w in range(NB)] for h in range(UNIT)]
        ids_row_in = [sem(f"ids_row_in{p}") for p in range(2)]
        dense_in = sem("dense_in")
        tile_begun = sem("tile_begun")
        held_in = [sem(f"held_in{o}") for o in range(NH)]
        weights_in = sem("weights_in")
        small_in = sem("small_in")
        cleared = sem("cleared")
        numbered = sem("numbered")
        held_high = sem("held_high")
        held_split = sem("held_split")
        w_high = sem("w_high")
        w_split = sem("w_split")
        hot_made = sem("hot_made")
        bank_full = sem("bank_full")
        act_out = sem("act_out")
        dve_out = sem("dve_out")
        gram_done = sem("gram_done")
        gram_act = sem("gram_act")
        gram_dve = sem("gram_dve")
        mid_done = sem("mid_done")
        mid_act = sem("mid_act")
        mid_dve = sem("mid_dve")
        z_done = sem("z_done")
        z_high = sem("z_high")
        z_low = sem("z_low")
        l1_done = sem("l1_done")
        h1_full = sem("h1_full")
        h1_high = sem("h1_high")
        h1_low = sem("h1_low")
        l2_done = sem("l2_done")
        h2_made = sem("h2_made")
        l3_done = sem("l3_done")
        y_made = sem("y_made")
        y_out = sem("y_out")
        block = ctx.enter_context(nc.Block())

        def reached(eng, s, value):
            if not isinstance(value, int) or value > 0:
                eng.wait_ge(s, value)

        def copied_out(eng, i, *bank):
            if bank in dve_nth:
                reached(eng, dve_out, i * NV + dve_nth[bank] + 1)
            else:
                reached(eng, act_out, i * NA + act_nth[bank] + 1)

        def mids_out(eng, j):
            eng.wait_ge(mid_act, (j + 1) * MA)
            eng.wait_ge(mid_dve, (j + 1) * MV)

        def mid_columns(m):
            first, count = MID[m]
            src = ps_mix[:, mix["mid", m], :].rearrange("p (j s f) -> p j s f", j=4, s=S)
            return [(tri[:, :, b * (b - 1) // 2:b * (b + 1) // 2], src[:, b - first, :, 0:b])
                    for b in range(max(first, 1), first + count)]

        BY_ACT = range(0, 3)
        BY_DVE = range(3, S)

        def products_out(eng, banks):
            reached(eng, gram_act, banks)
            reached(eng, gram_dve, banks)

        def own_block(k, s):
            src = ps_gram[s * FP:(s + 1) * FP, k % 2, 0:GB * S * F] \
                .rearrange("p (g s j) -> p g s j", g=GB, s=S)[:, :, s, :]
            return gram[s * FP:(s + 1) * FP, k * GB:(k + 1) * GB, :], src

        def feature_bank(u, kind, k):
            if kind == "rows":
                h, (first, n) = k // NB, BANKS[k % NB]
                src = ps_in[:, slot_of[u, kind, k], 0:n * TILE].rearrange("d (f b) -> d f b", f=n)
                return src, slice(first, first + n), slice(h * TILE, (h + 1) * TILE)
            if kind == "held":
                return ps_held[:, slot_of[u, kind, k], 0:UC].unsqueeze(1), slice(DENSE + 1 + k, DENSE + 2 + k), \
                    slice(0, UC)
            return ps_in[:, slot_of[u, kind, k], 0:UC].unsqueeze(1), slice(DENSE, DENSE + 1), slice(0, UC)

        def dense_cols(u):
            src = ps_in[:, slot_of[u, "dense", 0], 0:UC].rearrange("d (g s) -> d s g", s=S)
            return src, slice(u * (UC // S), (u + 1) * (UC // S))

        @block.sync
        def _(sp):
            def loads(i, u):
                n = i * UNITS + u
                for h in range(UNIT):
                    copied_out(sp, i - (u == 0), (u - 1) % UNITS, "rows", (h + 1) * NB - 1)
                    sp.dma_start(idx[:, h, :], ids[bass.ds((n * UNIT + h) * TILE, TILE), :]).then_inc(ids_in[h], 16)
                copied_out(sp, i - (u == 0), (u - 1) % UNITS, "dense", 0)
                sp.dma_start(dense[:], x[bass.ds(n * UC, UC), :].rearrange("(h p) d -> p h d", p=TILE)
                             ).then_inc(dense_in, 16)
                for o in range(NH):
                    reached(sp, hot_made, n * NH + o - (0 if NH % 2 and o == 0 else 1))
                    column = held[o][0]
                    sp.dma_start(ids_row[:, o % 2, :],
                                 ids_t[column:column + 1, bass.ds(n * UC, UC)].to_broadcast([HR, UC])
                                 ).then_inc(ids_row_in[o % 2], 16)

            def store(j):
                reached(sp, y_made, j + 1)
                sp.dma_start(out[0:1, bass.ds(j * COLS, COLS)], y[0:1, :]).then_inc(y_out, 16)

            for u in range(UNITS):
                loads(0, u)
            with sp.Fori(1, TURNS) as i:
                for u in range(UNITS):
                    loads(i, u)
                store(i - 1)
            store(TURNS - 1)
            sp.wait_ge(y_out, 16 * TURNS)

        @block.gpsimd
        def _(pool):
            nc.gpsimd.iota(row_ids[:], pattern=[[HR, HC]], base=0, channel_multiplier=1).then_inc(numbered, 1)
            pool.wait_ge(cleared, 1)
            nc.gpsimd.affine_select(out=ident[:], in_=ident[:], compare_op=ALU.not_equal, fill=1.0, base=0,
                                    pattern=[[-1, 128]], channel_multiplier=1).then_inc(numbered, 1)

            def gather(i):
                for u in range(UNITS):
                    for h in range(UNIT):
                        pool.wait_ge(ids_in[h], 16 * (i * UNITS + u + 1))
                        pool.sem_inc(tile_begun, 1)
                        for f, (column, table) in enumerate(gathered):
                            pool.indirect_dma_start(
                                emb[:, h, f, :], None, table,
                                bass.IndirectOffsetOnAxis(ap=idx[:, h, column:column + 1].bitcast(u32), axis=0),
                            ).then_inc(rows_in[h][f // 4], 16)

            gather(0)
            with pool.Fori(1, TURNS) as i:
                gather(i)

        @block.tensor
        def _(pe):
            def features(i, u, kind, k):
                bank = (u, kind, k)
                n = i * UNITS + u
                former, turn_before = before[bank]
                copied_out(pe, i + turn_before, *former)
                if kind == "rows":
                    h, w = k // NB, k % NB
                    first, count = BANKS[w]
                    pe.wait_ge(rows_in[h][w], 16 * count * (n + 1))
                    for f in range(count):
                        ins = nc.tensor.transpose(ps_in[:, slot_of[bank], f * TILE:(f + 1) * TILE],
                                                  emb[:, h, first + f, :], ident[:])
                elif kind == "held":
                    pe.wait_ge(hot_made, n * NH + k + 1)
                    if isinstance(i, int) and u == 0:
                        pe.wait_ge(held_split, k + 1)
                    for c in range(HC):
                        for part in (held_h, held_l):
                            ins = nc.tensor.matmul(ps_held[:, slot_of[bank], 0:UC], part[:, k, c, :], hot[:, k % 2, c, :],
                                                   start=c == 0 and part is held_h,
                                                   stop=c == HC - 1 and part is held_l)
                else:
                    pe.wait_ge(dense_in, 16 * (n + 1))
                    for h in range(UNIT):
                        ins = nc.tensor.transpose(ps_in[:, slot_of[bank], h * TILE:(h + 1) * TILE],
                                                  dense[:, h, :], ident[:])
                ins.then_inc(bank_full, 1)

            def products(i, u, b):
                if b % (BATCHES // UNIT) == 0:
                    h = b // (BATCHES // UNIT)
                    tile = [bank for bank in banks if bank[0] == u][:NB + NH + 1 + h * NB]
                    pe.wait_ge(act_out, i * NA + max(act_nth[x] for x in tile if x in act_nth) + 1)
                    pe.wait_ge(dve_out, i * NV + max(dve_nth[x] for x in tile if x in dve_nth) + 1)
                k = u * BATCHES + b
                products_out(pe, i * UNITS * BATCHES + k - 1)
                for g in range(GB):
                    b0 = (b * GB + g) * S
                    ins = nc.tensor.matmul(ps_gram[:, k % 2, g * S * F:(g + 1) * S * F],
                                           feat[:, b0:b0 + S, :], feat[:, b0:b0 + S, 0:F],
                                           start=True, stop=True)
                ins.then_inc(gram_done, 1)

            def layer(o, terms, done):
                for n, (w, v) in enumerate(terms):
                    ins = nc.tensor.matmul(o, w, v, start=n == 0, stop=n == len(terms) - 1)
                ins.then_inc(done, 1)

            def later(j, kind, k):
                o = ps_mix[:, mix[kind, k], :]
                if kind == "mid":
                    if k == 0:
                        products_out(pe, (j + 1) * UNITS * BATCHES)
                    if k >= 2 and k % 2:
                        pe.wait_ge(mid_dve, j * MV + k // 2)
                    elif k >= 2:
                        pe.wait_ge(mid_act, j * MA + k // 2)
                    first, count = MID[k]
                    for c in range(count):
                        ins = nc.tensor.transpose(o[:, c * 128:(c + 1) * 128], gram[:, :, first + c], ident[:])
                    ins.then_inc(mid_done, 1)
                elif kind == "z":
                    if k == 0:
                        mids_out(pe, j)
                    if k >= 2:
                        pe.wait_ge(z_low, j * ZC + k - 1)
                    for s in range(S):
                        ins = nc.tensor.transpose(o[:ZR, s * GROUPS:(s + 1) * GROUPS],
                                                  tri[:, s, k * ZR:(k + 1) * ZR], ident[:])
                    ins.then_inc(z_done, 1)
                elif kind == "l1":
                    if k == 0:
                        pe.wait_ge(z_low, (j + 1) * ZC)
                    if k >= 2:
                        pe.wait_ge(h1_high, j * N1 + k - 1)
                    n = slice(k * 128, (k + 1) * 128)
                    layer(o, [(w1d_h[:, n], den_h[:, :, :]), (w1d_h[:, n], den_l[:, :, :]),
                              (w1d_l[:, n], den_h[:, :, :])]
                          + [t for c in range(ZC) for t in ((w1z_h[:, c, n], z_h[:, c, :]),
                                                            (w1z_h[:, c, n], z_l[:, c, :]),
                                                            (w1z_l[:, c, n], z_h[:, c, :]))], l1_done)
                elif kind == "l2":
                    if k == 0:
                        pe.wait_ge(h1_low, (j + 1) * N1)
                    n = slice(k * 128, (k + 1) * 128)
                    layer(o, [t for c in range(N1) for t in ((w2_h[:, c, n], h1_h[:, c, :]),
                                                             (w2_h[:, c, n], h1_l[:, c, :]),
                                                             (w2_l[:, c, n], h1_h[:, c, :]))], l2_done)
                else:
                    pe.wait_ge(h2_made, (j + 1) * N2)
                    layer(o[0:1, :], [(w3_sb[:, c:c + 1], h2[:, c, :]) for c in range(N2)], l3_done)

            def turn(i, after):
                for u in range(UNITS):
                    for kind, k in steps(u, after):
                        if kind in ("rows", "held", "dense"):
                            features(i, u, kind, k)
                        elif kind == "gram":
                            products(i, u, k)
                        elif kind != "hot":
                            later(i - 1, kind, k)
                if after:
                    pe.wait_ge(y_made, i)

            pe.wait_ge(numbered, 2)
            pe.wait_ge(cleared, 2)
            turn(0, False)
            pe.wait_ge(w_split, 3)
            pe.wait_ge(small_in, 48)
            with pe.Fori(1, TURNS) as i:
                turn(i, True)
            for kind, k in mix_order:
                later(TURNS - 1, kind, k)

        @block.scalar
        def _(act):
            for o, (_, table) in enumerate(held):
                act.dma_start(held_raw[:, o, :, :], table.rearrange("(c p) d -> p c d", p=HR)
                              ).then_inc(held_in[o], 16)
            act.dma_start(w1z_raw[:], w1[0:PAIRS, :].rearrange("(c p) n -> p c n", p=ZR)).then_inc(weights_in, 16)
            act.dma_start(w1d_raw[:], w1[PAIRS:PAIRS + D, :]).then_inc(weights_in, 16)
            act.dma_start(w2_raw[:], w2.rearrange("(c p) n -> p c n", p=128)).then_inc(weights_in, 16)
            act.dma_start(w3_sb[:], w3[:, :]).then_inc(small_in, 16)
            act.dma_start(b1_sb[:], b1[:, :]).then_inc(small_in, 16)
            act.dma_start(b2_sb[:], b2[:, :]).then_inc(small_in, 16)
            for o in range(NH):
                act.wait_ge(held_in[o], 16)
                nc.scalar.copy(held_h[:, o, :, :], held_raw[:, o, :, :]).then_inc(held_high, 1)
            act.wait_ge(weights_in, 48)
            nc.scalar.copy(w1z_h[:], w1z_raw[:]).then_inc(w_high, 1)
            nc.scalar.copy(w1d_h[:], w1d_raw[:]).then_inc(w_high, 1)
            nc.scalar.copy(w2_h[:], w2_raw[:]).then_inc(w_high, 1)

            def features(i, u, kind, k):
                bank = (u, kind, k)
                if bank not in act_nth:
                    return
                act.wait_ge(bank_full, i * NE + nth[bank] + 1)
                if kind == "dense":
                    src, g = dense_cols(u)
                    nc.scalar.copy(den_h[:, :, g], src)
                src, f, b = feature_bank(u, kind, k)
                nc.scalar.copy(feat_v[:, f, b], src).then_inc(act_out, 1)

            def products(i, u, b):
                k = u * BATCHES + b
                act.wait_ge(gram_done, i * UNITS * BATCHES + k + 1)
                for s in BY_ACT:
                    ins = nc.scalar.copy(*own_block(k, s))
                ins.then_inc(gram_act, 1)

            def later(j, kind, k):
                src = ps_mix[:, mix[kind, k], :]
                if kind == "mid":
                    if k % 2 == 0:
                        act.wait_ge(mid_done, j * NM + k + 1)
                        for to, of in mid_columns(k):
                            ins = nc.scalar.copy(to, of)
                        ins.then_inc(mid_act, 1)
                elif kind == "z":
                    act.wait_ge(z_done, j * ZC + k + 1)
                    nc.scalar.copy(z_h[:, k, :], src[:ZR, :]).then_inc(z_high, 1)
                elif kind == "l1":
                    act.wait_ge(h1_full, j * N1 + k + 1)
                    nc.scalar.activation(h1_h[:, k, :], src, ACT.Relu, bias=b1_sb[:, k:k + 1]).then_inc(h1_high, 1)
                elif kind == "l2":
                    act.wait_ge(l2_done, j * N2 + k + 1)
                    nc.scalar.activation(h2[:, k, :], src, ACT.Relu, bias=b2_sb[:, k:k + 1]).then_inc(h2_made, 1)

            def turn(i, after):
                for u in range(UNITS):
                    for kind, k in steps(u, after):
                        if kind in ("rows", "held", "dense"):
                            features(i, u, kind, k)
                        elif kind == "gram":
                            products(i, u, k)
                        elif kind != "hot":
                            later(i - 1, kind, k)

            act.wait_ge(small_in, 48)
            turn(0, False)
            with act.Fori(1, TURNS) as i:
                turn(i, True)
            for kind, k in mix_order:
                later(TURNS - 1, kind, k)

        @block.vector
        def _(dve):
            nc.vector.memset(ident[:], 0.0).then_inc(cleared, 1)
            nc.vector.memset(feat_v[:, F:FP, :], 0.0).then_inc(cleared, 1)
            for o in range(NH):
                dve.wait_ge(held_high, o + 1)
                nc.vector.tensor_tensor(held_l[:, o, :, :], held_raw[:, o, :, :], held_h[:, o, :, :].bitcast(fp32),
                                        ALU.subtract).then_inc(held_split, 1)
            dve.wait_ge(w_high, 3)
            nc.vector.tensor_tensor(w1z_l[:], w1z_raw[:], w1z_h[:].bitcast(fp32), ALU.subtract).then_inc(w_split, 1)
            nc.vector.tensor_tensor(w1d_l[:], w1d_raw[:], w1d_h[:].bitcast(fp32), ALU.subtract).then_inc(w_split, 1)
            nc.vector.tensor_tensor(w2_l[:], w2_raw[:], w2_h[:].bitcast(fp32), ALU.subtract).then_inc(w_split, 1)

            def one_hot(i, u, o):
                n = i * UNITS + u
                uses = len(range(o % 2, NH, 2))
                dve.wait_ge(ids_row_in[o % 2], 16 * (n * uses + o // 2 + 1))
                if o >= 2:
                    reached(dve, bank_full, i * NE + nth[u, "held", o - 2] + 1)
                else:
                    last = NH - 2 + o if NH % 2 == 0 else NH - 1 - o
                    reached(dve, bank_full, (i - (u == 0)) * NE + nth[(u - 1) % UNITS, "held", last] + 1)
                nc.vector.tensor_tensor(hot[:, o % 2, :, :], bass.AP(ids_row, (o % 2) * UC, [[2 * UC, HR], [0, HC], [1, UC]]),
                                        bass.AP(row_ids, 0, [[HC, HR], [1, HC], [0, UC]]),
                                        ALU.is_equal).then_inc(hot_made, 1)

            def features(i, u, kind, k):
                bank = (u, kind, k)
                if bank not in dve_nth:
                    return
                if kind == "dense":
                    dve.wait_ge(act_out, i * NA + act_nth[bank] + 1)
                    src, g = dense_cols(u)
                    nc.vector.tensor_tensor(den_l[:, :, g], src, den_h[:, :, g].bitcast(fp32), ALU.subtract
                                            ).then_inc(dve_out, 1)
                else:
                    dve.wait_ge(bank_full, i * NE + nth[bank] + 1)
                    src, f, b = feature_bank(u, kind, k)
                    nc.vector.tensor_copy(feat_v[:, f, b], src).then_inc(dve_out, 1)

            def products(i, u, b):
                k = u * BATCHES + b
                dve.wait_ge(gram_done, i * UNITS * BATCHES + k + 1)
                for s in BY_DVE:
                    ins = nc.vector.tensor_copy(*own_block(k, s))
                ins.then_inc(gram_dve, 1)

            def h1_lower(j, k):
                dve.wait_ge(h1_high, j * N1 + k + 1)
                dve.wait_ge(h1_full, j * N1 + k + 1)
                nc.vector.tensor_tensor(h1_l[:, k, :], h1_x[:, k % 2, :], h1_h[:, k, :].bitcast(fp32),
                                        ALU.subtract).then_inc(h1_low, 1)

            def later(j, kind, k):
                src = ps_mix[:, mix[kind, k], :]
                if kind == "mid" and k % 2:
                    dve.wait_ge(mid_done, j * NM + k + 1)
                    for to, of in mid_columns(k):
                        ins = nc.vector.tensor_copy(to, of)
                    ins.then_inc(mid_dve, 1)
                elif kind == "z":
                    dve.wait_ge(z_high, j * ZC + k + 1)
                    nc.vector.tensor_tensor(z_l[:, k, :], src[:ZR, :], z_h[:, k, :].bitcast(fp32),
                                            ALU.subtract).then_inc(z_low, 1)
                elif kind == "l1":
                    dve.wait_ge(l1_done, j * N1 + k + 1)
                    if k >= 2:
                        dve.wait_ge(h1_low, j * N1 + k - 1)
                    nc.vector.tensor_scalar(h1_x[:, k % 2, :], src, b1_sb[:, k:k + 1], 0.0, ALU.add, ALU.max
                                            ).then_inc(h1_full, 1)
                    if k >= 1:
                        h1_lower(j, k - 1)
                    if k == N1 - 1:
                        h1_lower(j, k)
                elif kind == "l3":
                    dve.wait_ge(l3_done, j + 1)
                    nc.vector.tensor_copy(y[0:1, :].rearrange("o (g s) -> o s g", s=S),
                                          src[0:1, :].rearrange("o (s g) -> o s g", s=S)).then_inc(y_made, 1)

            def turn(i, after):
                for u in range(UNITS):
                    for kind, k in steps(u, after):
                        if kind == "hot":
                            one_hot(i, u, k)
                        elif kind in ("rows", "held", "dense"):
                            features(i, u, kind, k)
                        elif kind == "gram":
                            products(i, u, k)
                        else:
                            later(i - 1, kind, k)
                if after:
                    dve.wait_ge(y_out, 16 * i)

            dve.wait_ge(small_in, 48)
            dve.wait_ge(numbered, 2)
            turn(0, False)
            with dve.Fori(1, TURNS) as i:
                turn(i, True)
            for kind, k in mix_order:
                later(TURNS - 1, kind, k)


HELD = 7


def kernel(**inputs):
    import numpy as _np
    import concourse.bacc as _bacc
    from concourse import mybir as _mybir
    from concourse.bass_utils import run_bass_kernel_spmd as _run

    lay = {name: _np.asarray(a) for name, a in inputs.items()}
    nt = lay["ids"].shape[1]
    fewest = min(lay[f"tbl_{t}"].shape[0] for t in range(nt))
    held = [t for t in range(nt) if lay[f"tbl_{t}"].shape[0] == fewest][:HELD]
    gathered = [t for t in range(nt) if t not in held]

    place = gathered + [nt] + held
    row = {}
    for a in range(nt + 1):
        for b in range(a + 1, nt + 1):
            row[a, b] = len(row)
    order = [row[tuple(sorted((place[a], place[b])))] for b in range(nt + 1) for a in range(b)]
    order += list(range(len(row), lay["W_top1"].shape[0]))
    lay["W_top1"] = lay["W_top1"][order]
    lay["ids_t"] = lay["ids"].T
    for name in ("b_top1", "b_top2", "W_top3"):
        lay[name] = lay[name].reshape(-1, 128).T

    nc = _bacc.Bacc("TRN2", target_bir_lowering=False, num_devices=1)
    arrays, ap = {}, {}
    for name, a in lay.items():
        a = _np.ascontiguousarray(a)
        arrays[f"in_{name}"] = a
        ap[name] = nc.dram_tensor(f"in_{name}", a.shape, _mybir.dt.from_np(a.dtype), kind="ExternalInput").ap()
    rows = lay["r_dense_x"].shape[0]
    out = nc.dram_tensor("out_y", (1, rows), _mybir.dt.float32, kind="ExternalOutput").ap()
    dlrm_tower_kernel(nc, ap["r_dense_x"], ap["ids"], ap["ids_t"], [(t, ap[f"tbl_{t}"]) for t in gathered],
                      [(t, ap[f"tbl_{t}"]) for t in held], ap["W_top1"], ap["b_top1"], ap["W_top2"],
                      ap["b_top2"], ap["W_top3"], out)
    r = _run(nc, [arrays], core_ids=[0])
    return r.results[0]["out_y"].reshape(rows, 1)
```

```python
import concourse.bass as bass
from concourse import mybir
from contextlib import ExitStack


def dlrm_tower_kernel(nc, x_t, ids, ids_t, gathered, held, w1, b1, w2, b2, w3, out):
    fp32 = mybir.dt.float32
    f32r = mybir.dt.float32r
    i32 = mybir.dt.int32
    u32 = mybir.dt.uint32
    ALU = mybir.AluOpType
    ACT = mybir.ActivationFunctionType

    UC = x_t.shape[1]
    B, D = ids.shape[0], held[0][1].shape[1]
    NG, NH = len(gathered), len(held)
    F = NG + 1 + NH
    DENSE = NG
    TILE = 128
    UNIT = UC // TILE
    UNITS = B // UC
    FP = 32
    S = 4
    USED = (S - 1) * FP + F - 1
    FC = F - 1
    BANK = 512
    GB = 4
    BATCHES = UC // S // GB
    GROUPS = UC // S
    PAIRS = F * (F - 1) // 2
    ZC = 3
    ZR = PAIRS // ZC
    H1, H2 = w1.shape[1], w2.shape[1]
    N1, N2 = H1 // 128, H2 // 128
    ROWS = held[0][1].shape[0]
    HC = -(-ROWS // 128)
    HR = ROWS // HC
    BANKS = [(f, min(4, NG - f)) for f in range(0, NG, 4)]
    NB = len(BANKS)
    AT_ONCE = 128 // GROUPS
    MID = [(j, min(4 * AT_ONCE, F - j)) for j in range(1, F, 4 * AT_ONCE)]
    NM = len(MID)

    assert AT_ONCE == 2 and F % AT_ONCE == 1 and NM == 4 and N1 == 4 and N2 == 2
    assert ZC * ZR == PAIRS and HC * HR == ROWS

    def merged(*spans):
        at = [(start + (end - start) * (n + 0.5) / len(steps), m, n, step)
              for m, (steps, start, end) in enumerate(spans) for n, step in enumerate(steps)]
        return [step for *_, step in sorted(at)]

    half = BATCHES // UNIT

    needs = {c: next(m + 1 for m, (first, count) in enumerate(MID)
                     if (first + count) * (first + count - 1) // 2 >= (c + 1) * ZR) for c in range(ZC)}
    mix_order = [("mid", m) for m in range(NM)]
    for c in range(ZC):
        mix_order.insert(needs[c] + 1 + c, ("z", c))
    mix_order += [("l1", n) for n in range(N1)] + [("l2", n) for n in range(N2)] + [("l3", 0)]
    mix = {what: n % 2 for n, what in enumerate(mix_order)}
    assert len(mix_order) % 2 == 0 and ZC == 3

    def steps(later):
        pairs, l1, l2, l3 = ([step for step in mix_order if later and step[0] in kinds]
                             for kinds in (("mid", "z"), ("l1",), ("l2",), ("l3",)))
        rows = [("rows", w) for w in range(UNIT * NB)]
        held = [("held", o) for o in range(NH)]
        gram = [("gram", b) for b in range(BATCHES)]
        out = []
        for step in merged((rows[:NB], 0.05, 0.8), (held, 0, 1), ([("dense", 0)], 0.6, 0.8),
                           (pairs, 0.05, 0.6), (l1, 0.6, 0.95)):
            out.append(step)
            if step[0] == "held" and step[1] + 2 < NH:
                out.append(("hot", step[1] + 2))
        out += merged((rows[NB:], 0, 1), (gram[:half], 0.1, 1), (l2, 0, 0.5),
                      ([("next hot", 0), ("next hot", 1)], 0, 0.8))
        return out + [("parts", 0)] + merged((gram[half:], 0, 1), (l3, 0, 0.1))

    banks = [step for step in steps(False) if step[0] in ("rows", "held")]
    NE = len(banks)
    nth = {bank: e for e, bank in enumerate(banks)}
    rings = {"in": [b for b in banks if b[0] != "held"], "held": [b for b in banks if b[0] == "held"]}
    slot_of, before = {}, {}
    for ring in rings.values():
        for r, bank in enumerate(ring):
            slot_of[bank] = r % 2
        for r, bank in enumerate(ring):
            former = ring[r - 2] if r >= 2 else [other for other in ring if slot_of[other] == r % 2][-1]
            before[bank] = (former, -1 if r < 2 else 0)

    def by_vector(kind, k):
        return kind == "rows" and k >= NB and k % 2 == 1

    def blocks_by_vector(b):
        return range(2, S) if b >= half - 1 else range(0)

    act_nth, dve_nth = {}, {}
    for bank in [step for step in steps(False) if step in banks or step[0] == "dense"]:
        if not by_vector(*bank):
            act_nth[bank] = len(act_nth)
        else:
            dve_nth[bank] = len(dve_nth)
    NA, NV = len(act_nth), len(dve_nth)

    ctx = ExitStack()
    with ctx:
        def sb(name, shape, dt):
            return ctx.enter_context(nc.sbuf_tensor(name, shape, dt))

        def sem(name):
            return ctx.enter_context(nc.semaphore(name))

        sizes = [GROUPS * FC * 4, 2 * N1 * UC * 4, max(S * PAIRS, (2 + N2) * UC) * 4]
        at_gram = -(-nc.sbuf_base // 32) * 32
        sb("shared", [128, max(sum(sizes), NH * HC * D * 4) // 4], fp32)
        idx = sb("idx", [128, UNIT, NG + NH], i32)
        emb = sb("emb", [128, UNIT, NG, D], fp32)
        dense = sb("dense", [128, UC], fp32)
        ident = sb("ident", [128, 128], fp32)
        row_ids = sb("row_ids", [HR, HC], i32)
        ids_row = sb("ids_row", [HR, 2, UC], i32)
        hot = sb("hot", [HR, 2, HC, UC], f32r)
        held_h = sb("held_h", [HR, NH, HC, D], f32r)
        held_l = sb("held_l", [HR, NH, HC, D], f32r)
        feat = sb("feat", [128, UC, FP], fp32)
        feat_v = feat[:, :, :].rearrange("d b f -> d f b")
        den_h = sb("den_h", [128, S, GROUPS], f32r)
        den_l = sb("den_l", [128, S, GROUPS], f32r)
        z_h = sb("z_h", [ZR, ZC, UC], f32r)
        z_l = sb("z_l", [ZR, ZC, UC], f32r)
        y = sb("y", [1, B], fp32)
        w1z_h = sb("w1z_h", [ZR, ZC, H1], f32r)
        w1z_l = sb("w1z_l", [ZR, ZC, H1], f32r)
        w1d_h = sb("w1d_h", [128, H1], f32r)
        w1d_l = sb("w1d_l", [128, H1], f32r)
        w2_h = sb("w2_h", [128, N1, H2], f32r)
        w2_l = sb("w2_l", [128, N1, H2], f32r)
        w3_sb = sb("w3_sb", [128, N2], fp32)
        ones = sb("ones", [128, 1], fp32)
        b1_sb = sb("b1_sb", [128, N1], fp32)
        b2_sb = sb("b2_sb", [128, N2], fp32)

        at_h1, at_tri = (at_gram + sum(sizes[:n]) for n in (1, 2))
        placed = [at_gram, at_gram + max(sum(sizes), NH * HC * D * 4)]

        def place(name, shape, dt, at):
            size = 4
            for n in shape[1:]:
                size *= n
            assert placed[0] <= at and at + size <= placed[1]
            return nc.alloc_sbuf_tensor_at(name, shape, dt, offset=at)

        gram = place("gram", [128, FC, GROUPS], fp32, at_gram)
        h1_h = place("h1_h", [128, N1, UC], f32r, at_h1)
        h1_l = place("h1_l", [128, N1, UC], f32r, at_h1 + N1 * UC * 4)
        tri = place("tri", [GROUPS, S, PAIRS], fp32, at_tri)
        h1_x = place("h1_x", [128, 2, UC], fp32, at_tri)
        h2 = place("h2", [128, N2, UC], fp32, at_tri + 2 * UC * 4)
        held_raw = place("held_raw", [HR, NH, HC, D], fp32, at_gram)
        w1z_raw = sb("w1z_raw", [ZR, ZC, H1], fp32)
        w1d_raw = sb("w1d_raw", [128, H1], fp32)
        w2_raw = sb("w2_raw", [128, N1, H2], fp32)
        weight_parts = [tuple(w[:, c, :] for w in (w1z_raw, w1z_h, w1z_l)) for c in range(ZC)]
        weight_parts += [tuple(w[:] for w in (w1d_raw, w1d_h, w1d_l))]
        weight_parts += [tuple(w[:, c:c + 2, :] for w in (w2_raw, w2_h, w2_l)) for c in range(0, N1, 2)]

        def ps(name, shape):
            return ctx.enter_context(nc.psum_tensor(name, shape, fp32))

        ps_in = ps("ps_in", [128, 2, BANK])
        ps_held = ps("ps_held", [128, 2, BANK])
        ps_gram = ps("ps_gram", [128, 2, BANK])
        ps_mix = ps("ps_mix", [128, 2, BANK])

        ids_in = [sem(f"ids_in{h}") for h in range(UNIT)]
        rows_in = [[sem(f"rows_in{h}_{w}") for w in range(NB)] for h in range(UNIT)]
        ids_row_in = [sem(f"ids_row_in{p}") for p in range(2)]
        dense_in = sem("dense_in")
        tile_begun = sem("tile_begun")
        turning = sem("turning")
        held_in = [sem(f"held_in{o}") for o in range(NH)]
        weights_in = sem("weights_in")
        small_in = sem("small_in")
        cleared = sem("cleared")
        numbered = sem("numbered")
        held_high = sem("held_high")
        held_split = sem("held_split")
        w_high = sem("w_high")
        w_split = sem("w_split")
        hot_made = sem("hot_made")
        bank_full = sem("bank_full")
        act_out = sem("act_out")
        dve_out = sem("dve_out")
        gram_done = sem("gram_done")
        gram_act = sem("gram_act")
        gram_dve = sem("gram_dve")
        dense_high = sem("dense_high")
        dense_low = sem("dense_low")
        mid_done = sem("mid_done")
        mid_out = sem("mid_out")
        mid_dve = sem("mid_dve")
        z_done = sem("z_done")
        z_high = sem("z_high")
        z_low = sem("z_low")
        l1_done = sem("l1_done")
        h1_full = sem("h1_full")
        h1_high = sem("h1_high")
        h1_low = sem("h1_low")
        l2_done = sem("l2_done")
        h2_made = sem("h2_made")
        first_weighed = sem("first_weighed")
        weighed = sem("weighed")
        l3_done = sem("l3_done")
        y_made = sem("y_made")
        y_out = sem("y_out")
        block = ctx.enter_context(nc.Block())

        def reached(eng, s, value):
            if not isinstance(value, int) or value > 0:
                eng.wait_ge(s, value)

        def copied_out(eng, i, *bank):
            if bank in dve_nth:
                reached(eng, dve_out, i * NV + dve_nth[bank] + 1)
            else:
                reached(eng, act_out, i * NA + act_nth[bank] + 1)

        last_bank = {("mid", 0): (ps_mix, 0), ("mid", 1): (ps_mix, 1), ("mid", 2): (ps_mix, 0), ("mid", 3): (ps_mix, 1),
                     ("z", 0): (ps_gram, 0), ("z", 1): (ps_gram, 1), ("z", 2): (ps_mix, 0),
                     ("l1", 0): (ps_in, 0), ("l1", 1): (ps_in, 1), ("l1", 2): (ps_held, 0), ("l1", 3): (ps_held, 1),
                     ("l2", 0): (ps_gram, 0), ("l2", 1): (ps_gram, 1), ("l3", 0): (ps_mix, 1)}
        last_order = [("mid", m) for m in range(NM)] + [step for step in mix_order if step[0] != "mid"]

        def is_last(j):
            return isinstance(j, int) and j == UNITS - 1

        def bank_of(j, kind, k, size):
            ps, slot = last_bank[kind, k] if is_last(j) else (ps_mix, mix[kind, k])
            return ps[:, slot, 0:size]

        def mid_columns(j, m):
            first, count = MID[m]
            src = bank_of(j, "mid", m, BANK).rearrange("p (t s f) -> p t s f", t=4, s=S)
            return [(tri[:, :, b * (b - 1) // 2:b * (b + 1) // 2],
                     src[(b - first) % AT_ONCE * GROUPS:((b - first) % AT_ONCE + 1) * GROUPS, (b - first) // AT_ONCE, :, 0:b])
                    for b in range(first, first + count)]

        GV = sum(len(blocks_by_vector(b)) > 0 for b in range(BATCHES))

        def products_out(eng, n, b):
            reached(eng, gram_act, n * BATCHES + b + 1)
            if blocks_by_vector(b):
                reached(eng, gram_dve, n * GV + sum(len(blocks_by_vector(c)) > 0 for c in range(b)) + 1)

        def own_block(k, s):
            end = min((s + 1) * FP, USED)
            src = ps_gram[s * FP:end, k % 2, 0:GB * S * FC] \
                .rearrange("p (g s j) -> p g s j", g=GB, s=S)[:, :, s, :]
            return gram[s * FP:end, :, k * GB:(k + 1) * GB].rearrange("p j g -> p g j"), src

        def feature_bank(kind, k):
            if kind == "rows":
                h, (first, n) = k // NB, BANKS[k % NB]
                src = ps_in[:, slot_of[kind, k], 0:n * TILE].rearrange("d (f b) -> d f b", f=n)
                return src, slice(first, first + n), slice(h * TILE, (h + 1) * TILE)
            if kind == "held":
                return ps_held[:, slot_of[kind, k], 0:UC].unsqueeze(1), slice(DENSE + 1 + k, DENSE + 2 + k), \
                    slice(0, UC)
            return dense[:].unsqueeze(1), slice(DENSE, DENSE + 1), slice(0, UC)

        def dense_cols():
            return dense[:].rearrange("d (g s) -> d s g", s=S)

        @block.sync
        def _(sp):
            def weights():
                sp.dma_start(w1z_raw[:], w1[0:PAIRS, :].rearrange("(c p) n -> p c n", p=ZR)).then_inc(weights_in, 16)
                sp.dma_start(w1d_raw[:], w1[PAIRS:PAIRS + D, :]).then_inc(weights_in, 16)
                sp.dma_start(w2_raw[:], w2.rearrange("(c p) n -> p c n", p=128)).then_inc(weights_in, 16)
                sp.dma_start(w3_sb[:], w3[:, :]).then_inc(small_in, 16)
                sp.dma_start(b1_sb[:], b1[:, :]).then_inc(small_in, 16)
                sp.dma_start(b2_sb[:], b2[:, :]).then_inc(small_in, 16)

            def load_idx(i, h):
                reached(sp, bank_full, (i - 1) * NE + nth["rows", (h + 1) * NB - 1] + 1)
                sp.dma_start(idx[:, h, :], ids[bass.ds((i * UNIT + h) * TILE, TILE), :]).then_inc(ids_in[h], 16)

            def load_dense(i):
                reached(sp, dense_low, i)
                sp.dma_start(dense[:], x_t[bass.ds(i * D, D), :]).then_inc(dense_in, 16)

            def load_ids_row(i, o):
                if not (NH % 2 and o == 1):
                    reached(sp, hot_made, i * NH + o - (0 if NH % 2 and o == 0 else 1))
                column = held[o][0]
                sp.dma_start(ids_row[:, o % 2, :],
                             ids_t[column:column + 1, bass.ds(i * UC, UC)].to_broadcast([HR, UC])
                             ).then_inc(ids_row_in[o % 2], 16)

            def loads(i):
                load_idx(i, 0)
                load_ids_row(i, 0)
                load_ids_row(i, 1)
                load_dense(i)
                load_idx(i, 1)
                for o in range(2, NH):
                    load_ids_row(i, o)
                    if o == min(5, NH - 1) and isinstance(i, int):
                        weights()

            loads(0)
            with sp.Fori(1, UNITS) as i:
                loads(i)

        @block.gpsimd
        def _(pool):
            nc.gpsimd.iota(row_ids[:], pattern=[[HR, HC]], base=0, channel_multiplier=1).then_inc(numbered, 1)
            pool.wait_ge(cleared, 1)
            nc.gpsimd.affine_select(out=ident[:], in_=ident[:], compare_op=ALU.not_equal, fill=1.0, base=0,
                                    pattern=[[-1, 128]], channel_multiplier=1).then_inc(numbered, 1)

            def gather(i):
                for h in range(UNIT):
                    reached(pool, bank_full, (i - 1) * NE + nth["rows", (h + 1) * NB - 1] + 1)
                    pool.wait_ge(ids_in[h], 16 * (i + 1))
                    pool.sem_inc(tile_begun, 1)
                    for f, (column, table) in enumerate(gathered):
                        pool.indirect_dma_start(
                            emb[:, h, f, :], None, table,
                            bass.IndirectOffsetOnAxis(ap=idx[:, h, column:column + 1].bitcast(u32), axis=0),
                        ).then_inc(rows_in[h][f // 4], 16)

            gather(0)
            with pool.Fori(1, UNITS) as i:
                gather(i)

        @block.tensor
        def _(pe):
            def features(i, kind, k):
                bank = (kind, k)
                former, unit_before = before[bank]
                copied_out(pe, i + unit_before, *former)
                if kind == "rows":
                    h, w = k // NB, k % NB
                    first, count = BANKS[w]
                    pe.wait_ge(rows_in[h][w], 16 * count * (i + 1))
                    for f in range(count):
                        ins = nc.tensor.transpose(ps_in[:, slot_of[bank], f * TILE:(f + 1) * TILE],
                                                  emb[:, h, first + f, :], ident[:])
                else:
                    pe.wait_ge(hot_made, i * NH + k + 1)
                    if isinstance(i, int):
                        pe.wait_ge(held_split, k + 1)
                    for c in range(HC):
                        for part in (held_h, held_l):
                            ins = nc.tensor.matmul(ps_held[:, slot_of[bank], 0:UC], part[:, k, c, :], hot[:, k % 2, c, :],
                                                   start=c == 0 and part is held_h,
                                                   stop=c == HC - 1 and part is held_l)
                ins.then_inc(bank_full, 1)

            def products(i, b):
                if b % (BATCHES // UNIT) == 0:
                    h = b // (BATCHES // UNIT)
                    tile = banks[:NB + NH + h * NB] + [("dense", 0)]
                    for out_of, count, nths in ((act_out, NA, act_nth), (dve_out, NV, dve_nth)):
                        mine = [nths[bank] for bank in tile if bank in nths]
                        if mine:
                            pe.wait_ge(out_of, i * count + max(mine) + 1)
                products_out(pe, i - (b < 2), (b - 2) % BATCHES)
                for g in range(GB):
                    b0 = (b * GB + g) * S
                    ins = nc.tensor.matmul(ps_gram[0:USED, b % 2, g * S * FC:(g + 1) * S * FC],
                                           feat[:, b0:b0 + S, :].rearrange("d s f -> d (s f)")[:, 0:USED],
                                           feat[:, b0:b0 + S, 1:F],
                                           start=True, stop=True)
                ins.then_inc(gram_done, 1)

            def three(w_high, w_low, v_high, v_low):
                return [(w_high, v_high), (w_high, v_low), (w_low, v_high)]

            def l2_terms(k, c):
                n = slice(k * 128, (k + 1) * 128)
                return three(w2_h[:, c, n], w2_l[:, c, n], h1_h[:, c, :], h1_l[:, c, :])

            def l1_chunk(j, k, c):
                n = slice(k * 128, (k + 1) * 128)
                if c == 0:
                    terms = three(w1d_h[:, n], w1d_l[:, n], den_h[:, :, :], den_l[:, :, :])
                else:
                    terms = three(w1z_h[:, c - 1, n], w1z_l[:, c - 1, n], z_h[:, c - 1, :], z_l[:, c - 1, :])
                for m, term in enumerate(terms):
                    ins = nc.tensor.matmul(bank_of(j, "l1", k, UC), *term, start=c == 0 and m == 0,
                                           stop=c == ZC and m == 2)
                if c == ZC:
                    ins.then_inc(l1_done, 1)

            def bank_free(j, what):
                place = mix_order.index(what)
                if place >= 2:
                    kind, k = mix_order[place - 2]
                    out_of, count = {"mid": (mid_out, NM), "z": (z_low, ZC), "l1": (h1_high, N1),
                                     "l2": (h2_made, N2)}[kind]
                    pe.wait_ge(out_of, j * count + k + 1)

            def later(j, kind, k):
                o = bank_of(j, kind, k, UC if kind != "mid" else BANK)
                if not is_last(j):
                    bank_free(j, (kind, k))
                if kind == "mid":
                    if k == 0:
                        products_out(pe, j, BATCHES - 1)
                    if is_last(j) and k >= 2:
                        pe.wait_ge(*((mid_dve, 1) if k % 2 else (mid_out, j * NM + 1)))
                    first, count = MID[k]
                    for t in range(count // AT_ONCE):
                        ins = nc.tensor.transpose(o[:, t * 128:t * 128 + USED],
                                                  gram[0:USED, first - 1 + t * AT_ONCE:first - 1 + (t + 1) * AT_ONCE, :],
                                                  ident[0:USED, 0:USED])
                    ins.then_inc(mid_done, 1)
                elif kind == "z":
                    if is_last(j):
                        pe.wait_ge(mid_out, j * NM + (needs[k] + 1) // 2)
                        pe.wait_ge(mid_dve, needs[k] // 2)
                    else:
                        pe.wait_ge(mid_out, j * NM + needs[k])
                    pe.sem_inc(turning, 1)
                    for s in range(S):
                        ins = nc.tensor.transpose(o[:ZR, s * GROUPS:(s + 1) * GROUPS],
                                                  tri[:, s, k * ZR:(k + 1) * ZR], ident[:GROUPS, :GROUPS])
                    ins.then_inc(z_done, 1)
                elif kind == "l1":
                    if k == 0:
                        pe.wait_ge(dense_low, j + 1)
                    for c in range(ZC + 1):
                        if k == 0 and c > 0:
                            pe.wait_ge(z_low, j * ZC + c)
                        l1_chunk(j, k, c)
                elif kind == "l2":
                    for c in range(N1 - 1):
                        if k == 0:
                            pe.wait_ge(h1_low, j * N1 + c + 1)
                        for m, term in enumerate(l2_terms(k, c)):
                            nc.tensor.matmul(o, *term, start=c == 0 and m == 0, stop=False)
                    if k == N2 - 1:
                        pe.wait_ge(h1_low, (j + 1) * N1)
                        for other in range(N2):
                            for m, term in enumerate(l2_terms(other, N1 - 1)):
                                ins = nc.tensor.matmul(bank_of(j, "l2", other, UC), *term, start=False, stop=m == 2)
                            ins.then_inc(l2_done, 1)
                elif is_last(j):
                    for c in range(N2):
                        pe.wait_ge(h2_made, j * N2 + c + 1)
                        ins = nc.tensor.matmul(o[0:1, :], w3_sb[:, c:c + 1], h2[:, c, :], start=c == 0, stop=c == N2 - 1)
                    ins.then_inc(l3_done, 1)
                else:
                    pe.wait_ge(weighed, j + 1)
                    nc.tensor.matmul(o[0:1, :], ones[:], h1_x[:, 1, :], start=True, stop=True).then_inc(l3_done, 1)

            def unit(i, after):
                for kind, k in steps(after):
                    if kind in ("rows", "held"):
                        features(i, kind, k)
                    elif kind == "gram":
                        products(i, k)
                    elif kind not in ("dense", "parts", "hot", "next hot"):
                        later(i - 1, kind, k)
                if after:
                    pe.wait_ge(y_made, i)

            pe.wait_ge(numbered, 2)
            pe.wait_ge(cleared, 3)
            unit(0, False)
            pe.wait_ge(w_split, len(weight_parts))
            pe.wait_ge(small_in, 48)
            with pe.Fori(1, UNITS) as i:
                unit(i, True)
            j = UNITS - 1
            pe.wait_ge(dense_low, j + 1)
            for n in range(0, N1 // 2):
                l1_chunk(j, n, 0)
            for m in range(2):
                later(j, "mid", m)
            for n in range(N1 // 2, N1):
                l1_chunk(j, n, 0)
            for m in range(2, NM):
                later(j, "mid", m)
            for c in range(ZC):
                later(j, "z", c)
            pe.wait_ge(z_low, j * ZC + 1)
            for n in range(N1):
                l1_chunk(j, n, 1)
            for n in range(N1):
                for c in range(1, ZC):
                    if n == 0:
                        pe.wait_ge(z_low, j * ZC + c + 1)
                    l1_chunk(j, n, c + 1)
            for n in range(N2):
                later(j, "l2", n)
            later(j, "l3", 0)

        @block.scalar
        def _(act):
            def load_table(o):
                if o < NH:
                    act.dma_start(held_raw[:, o, :, :], held[o][1].rearrange("(c p) d -> p c d", p=HR)
                                  ).then_inc(held_in[o], 16)

            AHEAD = 3
            for o in range(AHEAD):
                load_table(o)

            def table_high(o):
                load_table(o + AHEAD)
                act.wait_ge(held_in[o], 16)
                nc.scalar.copy(held_h[:, o, :, :], held_raw[:, o, :, :]).then_inc(held_high, 1)

            def weights_high(n):
                if n == 0:
                    act.wait_ge(weights_in, 48)
                raw, high, _ = weight_parts[n]
                nc.scalar.copy(high, raw).then_inc(w_high, 1)

            def features(i, kind, k):
                bank = (kind, k)
                if bank not in act_nth:
                    return
                if kind == "dense":
                    act.wait_ge(dense_in, 16 * (i + 1))
                else:
                    act.wait_ge(bank_full, i * NE + nth[bank] + 1)
                src, f, b = feature_bank(kind, k)
                nc.scalar.copy(feat_v[:, f, b], src).then_inc(act_out, 1)

            def dense_part(i):
                reached(act, l1_done, i * N1)
                nc.scalar.copy(den_h[:], dense_cols()).then_inc(dense_high, 1)

            def products(i, b):
                act.wait_ge(gram_done, i * BATCHES + b + 1)
                for s in range(S):
                    if s not in blocks_by_vector(b):
                        ins = nc.scalar.copy(*own_block(b, s))
                ins.then_inc(gram_act, 1)

            def later(j, kind, k):
                src = bank_of(j, kind, k, UC)
                if kind == "mid":
                    if not is_last(j) or k % 2 == 0:
                        act.wait_ge(mid_done, j * NM + k + 1)
                        for to, of in mid_columns(j, k):
                            ins = nc.scalar.copy(to, of)
                        ins.then_inc(mid_out, 1)
                elif kind == "z":
                    act.wait_ge(z_done, j * ZC + k + 1)
                    nc.scalar.copy(z_h[:, k, :], src[:ZR, :]).then_inc(z_high, 1)
                elif kind == "l1":
                    act.wait_ge(h1_full, j * N1 + k + 1)
                    nc.scalar.activation(h1_h[:, k, :], src, ACT.Relu, bias=b1_sb[:, k:k + 1]).then_inc(h1_high, 1)
                elif kind == "l2" and k == N2 - 1:
                    for n in range(N2):
                        act.wait_ge(l2_done, j * N2 + n + 1)
                        nc.scalar.activation(h2[:, n, :], bank_of(j, "l2", n, UC), ACT.Relu,
                                             bias=b2_sb[:, n:n + 1]).then_inc(h2_made, 1)

            def unit(i, after):
                for kind, k in steps(after):
                    if kind in ("rows", "held", "dense"):
                        features(i, kind, k)
                    elif kind == "gram":
                        products(i, k)
                        if not after and k == 0:
                            for n in range(len(weight_parts)):
                                weights_high(n)
                    elif kind == "parts":
                        dense_part(i)
                    elif "hot" not in kind:
                        later(i - 1, kind, k)
                    elif kind == "hot" and not after:
                        table_high(k)

            for o in range(2):
                table_high(o)
            unit(0, False)
            act.wait_ge(small_in, 48)
            with act.Fori(1, UNITS) as i:
                unit(i, True)
            for kind, k in last_order:
                later(UNITS - 1, kind, k)
            act.wait_ge(y_made, UNITS)
            act.dma_start(out[:], y[0:1, :]).then_inc(y_out, 16)
            act.wait_ge(y_out, 16)

        @block.vector
        def _(dve):
            nc.vector.memset(ident[:], 0.0).then_inc(cleared, 1)
            nc.vector.memset(feat_v[:, F:FP, :], 0.0).then_inc(cleared, 1)
            nc.vector.memset(ones[:], 1.0).then_inc(cleared, 1)

            def table_low(o):
                dve.wait_ge(held_high, o + 1)
                nc.vector.tensor_tensor(held_l[:, o, :, :], held_raw[:, o, :, :], held_h[:, o, :, :].bitcast(fp32),
                                        ALU.subtract).then_inc(held_split, 1)

            def weights_low(n):
                dve.wait_ge(w_high, n + 1)
                raw, high, low = weight_parts[n]
                nc.vector.tensor_tensor(low, raw, high.bitcast(fp32), ALU.subtract).then_inc(w_split, 1)

            def one_hot(i, o):
                uses = len(range(o % 2, NH, 2))
                dve.wait_ge(ids_row_in[o % 2], 16 * (i * uses + o // 2 + 1))
                if o >= 2:
                    reached(dve, bank_full, i * NE + nth["held", o - 2] + 1)
                else:
                    last = NH - 2 + o if NH % 2 == 0 else NH - 1 - o
                    reached(dve, bank_full, (i - 1) * NE + nth["held", last] + 1)
                nc.vector.tensor_tensor(hot[:, o % 2, :, :], bass.AP(ids_row, (o % 2) * UC, [[2 * UC, HR], [0, HC], [1, UC]]),
                                        bass.AP(row_ids, 0, [[HC, HR], [1, HC], [0, UC]]),
                                        ALU.is_equal).then_inc(hot_made, 1)

            def features(i, kind, k):
                bank = (kind, k)
                if bank not in dve_nth:
                    return
                dve.wait_ge(bank_full, i * NE + nth[bank] + 1)
                src, f, b = feature_bank(kind, k)
                nc.vector.tensor_copy(feat_v[:, f, b], src).then_inc(dve_out, 1)

            def dense_part(i):
                dve.wait_ge(dense_high, i + 1)
                nc.vector.tensor_tensor(den_l[:], dense_cols(), den_h[:].bitcast(fp32), ALU.subtract
                                        ).then_inc(dense_low, 1)

            def products(i, b):
                if not blocks_by_vector(b):
                    return
                dve.wait_ge(gram_done, i * BATCHES + b + 1)
                for s in blocks_by_vector(b):
                    ins = nc.vector.tensor_copy(*own_block(b, s))
                ins.then_inc(gram_dve, 1)

            def weigh(j):
                dve.wait_ge(h1_low, (j + 1) * N1)
                dve.wait_ge(h2_made, (j + 1) * N2)
                nc.vector.tensor_scalar(h1_x[:, 0, :], h2[:, 0, :], w3_sb[:, 0:1], None, ALU.mult
                                        ).then_inc(first_weighed, 1)
                dve.wait_ge(first_weighed, j + 1)
                nc.vector.scalar_tensor_tensor(h1_x[:, 1, :], h2[:, 1, :], w3_sb[:, 1:2], h1_x[:, 0, :],
                                               ALU.mult, ALU.add).then_inc(weighed, 1)

            def h1_lower(j, k):
                dve.wait_ge(h1_high, j * N1 + k + 1)
                dve.wait_ge(h1_full, j * N1 + k + 1)
                nc.vector.tensor_tensor(h1_l[:, k, :], h1_x[:, k % 2, :], h1_h[:, k, :].bitcast(fp32),
                                        ALU.subtract).then_inc(h1_low, 1)

            def later(j, kind, k):
                src = bank_of(j, kind, k, UC)
                if kind == "mid" and is_last(j) and k % 2:
                    dve.wait_ge(mid_done, j * NM + k + 1)
                    for to, of in mid_columns(j, k):
                        ins = nc.vector.tensor_copy(to, of)
                    ins.then_inc(mid_dve, 1)
                elif kind == "z":
                    dve.wait_ge(z_high, j * ZC + k + 1)
                    nc.vector.tensor_tensor(z_l[:, k, :], src[:ZR, :], z_h[:, k, :].bitcast(fp32),
                                            ALU.subtract).then_inc(z_low, 1)
                elif kind == "l1":
                    dve.wait_ge(l1_done, j * N1 + k + 1)
                    if k >= 2:
                        dve.wait_ge(h1_low, j * N1 + k - 1)
                    nc.vector.tensor_scalar(h1_x[:, k % 2, :], src, b1_sb[:, k:k + 1], 0.0, ALU.add, ALU.max
                                            ).then_inc(h1_full, 1)
                    if k >= 1:
                        h1_lower(j, k - 1)
                    if k == N1 - 1:
                        h1_lower(j, k)
                elif kind == "l3":
                    dve.wait_ge(l3_done, j + 1)
                    nc.vector.tensor_copy(y[0:1, bass.ds(j * UC, UC)].rearrange("o (g s) -> o s g", s=S),
                                          src[0:1, :].rearrange("o (s g) -> o s g", s=S)).then_inc(y_made, 1)

            def unit(i, after, following=True):
                for kind, k in steps(after):
                    if kind == "hot":
                        one_hot(i, k)
                        if not after:
                            table_low(k)
                    elif kind == "next hot":
                        if following:
                            one_hot(i + 1, k)
                    elif kind in ("rows", "held", "dense"):
                        features(i, kind, k)
                    elif kind == "parts":
                        dense_part(i)
                    elif kind == "gram":
                        products(i, k)
                        if after and k == half - 2:
                            weigh(i - 1)
                        if not after and k < len(weight_parts) // 2:
                            weights_low(2 * k)
                            weights_low(2 * k + 1)
                    else:
                        later(i - 1, kind, k)

            dve.wait_ge(numbered, 1)
            for o in range(2):
                one_hot(0, o)
                table_low(o)
            unit(0, False)
            dve.wait_ge(small_in, 48)
            with dve.Fori(1, UNITS - 1) as i:
                unit(i, True)
            unit(UNITS - 1, True, following=False)
            for kind, k in last_order:
                later(UNITS - 1, kind, k)


SAMPLES = 256
HELD = 7


def kernel(**inputs):
    import numpy as _np
    import concourse.bacc as _bacc
    from concourse import mybir as _mybir
    from concourse.bass_utils import run_bass_kernel_spmd as _run

    lay = {name: _np.asarray(a) for name, a in inputs.items()}
    nt = lay["ids"].shape[1]
    fewest = min(lay[f"tbl_{t}"].shape[0] for t in range(nt))
    held = [t for t in range(nt) if lay[f"tbl_{t}"].shape[0] == fewest][:HELD]
    gathered = [t for t in range(nt) if t not in held]

    place = gathered + [nt] + held
    row = {}
    for a in range(nt + 1):
        for b in range(a + 1, nt + 1):
            row[a, b] = len(row)
    order = [row[tuple(sorted((place[a], place[b])))] for b in range(nt + 1) for a in range(b)]
    order += list(range(len(row), lay["W_top1"].shape[0]))
    lay["W_top1"] = lay["W_top1"][order]
    lay["ids_t"] = lay["ids"].T
    dim = lay["r_dense_x"].shape[1]
    lay["dense_t"] = lay.pop("r_dense_x").reshape(-1, SAMPLES, dim).transpose(0, 2, 1).reshape(-1, SAMPLES)
    for name in ("b_top1", "b_top2", "W_top3"):
        lay[name] = lay[name].reshape(-1, 128).T

    nc = _bacc.Bacc("TRN2", target_bir_lowering=False, num_devices=1)
    arrays, ap = {}, {}
    for name, a in lay.items():
        a = _np.ascontiguousarray(a)
        arrays[f"in_{name}"] = a
        ap[name] = nc.dram_tensor(f"in_{name}", a.shape, _mybir.dt.from_np(a.dtype), kind="ExternalInput").ap()
    rows = lay["ids"].shape[0]
    out = nc.dram_tensor("out_y", (1, rows), _mybir.dt.float32, kind="ExternalOutput").ap()
    dlrm_tower_kernel(nc, ap["dense_t"], ap["ids"], ap["ids_t"], [(t, ap[f"tbl_{t}"]) for t in gathered],
                      [(t, ap[f"tbl_{t}"]) for t in held], ap["W_top1"], ap["b_top1"], ap["W_top2"],
                      ap["b_top2"], ap["W_top3"], out)
    r = _run(nc, [arrays], core_ids=[0])
    return r.results[0]["out_y"].reshape(rows, 1)
```
